# Optimizing a Trainium2 kernel written in Bass

```python
import numpy as np
import jax
import jax.numpy as jnp

def _softmax(x, axis=-1):
    return jax.nn.softmax(x, axis=axis)

def _gelu(x):
    return jax.nn.gelu(x, approximate=True)

def _silu(x):
    return jax.nn.silu(x)

def _sigmoid(x):
    return jax.nn.sigmoid(x)

def _layernorm(x, axis=-1, eps=1e-05):
    m = jnp.mean(x, axis=axis, keepdims=True)
    v = jnp.var(x, axis=axis, keepdims=True)
    return (x - m) / jnp.sqrt(v + eps)

def _scatter_add(tgt, idx, src, axis=0):
    return tgt.at[idx].add(src)

def _segment_sum(src, seg, n):
    return jax.ops.segment_sum(src, seg, n)
kernel_name = 'mk_adj_preln_d2_adj_r2_ccfe8d'

def setup_inputs(seed: int=0):
    np.random.seed(seed)
    _w = jnp.asarray

    def _rec_inputs():
        import jax
        import jax.numpy as jnp
        _gk = jax.random.key(seed)
        x = 7.22e-05 + 1 * jax.random.normal(jax.random.fold_in(_gk, 1), (16, 512, 256), jnp.float32)
        _w = (1.0 + jnp.arange(512, dtype=jnp.float32)) ** (-0.5)
        _w = _w / _w.mean()
        _pij = jnp.clip(0.0078125 * _w[:, None] * _w[None, :], 0.0, 1.0)
        _a = jax.random.uniform(jax.random.fold_in(_gk, 2), (16, 512, 512)) < _pij
        _a = jnp.logical_or(_a, jnp.swapaxes(_a, -1, -2))
        _a = jnp.logical_or(_a, jnp.eye(512, dtype=bool))
        _af = _a.astype(jnp.float32)
        _af = _af * jax.random.uniform(jax.random.fold_in(_gk, 3), (16, 512, 512), jnp.float32, 0.05, 1)
        adj = _af
        _nm = jnp.ones((16, 512), dtype=bool)
        nodemask = _nm
        return (x, adj, nodemask)
    x, adj, nodemask = _rec_inputs()

    def _L0_gnn_setup():
        import jax, jax.numpy as jnp
        import numpy as np
        key = jax.random.key(seed)
        k1, k2, k3 = jax.random.split(key, 3)
        B, N, F, D = (8, 1024, 256, 256)
        x = jax.random.normal(k1, (B, N, F), dtype=jnp.float32)
        a = jax.random.uniform(k2, (B, N, N), dtype=jnp.float32)
        kernel = jax.random.normal(k3, (F, D), dtype=jnp.float32) * (1.0 / np.sqrt(F))
        return {'x': x, 'a': a, 'kernel': kernel}
    _L0_gnn_all = _L0_gnn_setup()
    _L0_gnn_in = {k: v for k, v in _L0_gnn_all.items() if k in ('kernel',)}
    del _L0_gnn_all

    def _L1_gnn_setup():
        import jax, jax.numpy as jnp
        import numpy as np
        HEADS = 8
        DIM_HEAD = 64
        LA = 0.33
        LD = 0.33
        LG = 0.33
        key = jax.random.key(seed)
        ks = jax.random.split(key, 6)
        B, N, D = (4, 512, 256)
        inner = HEADS * DIM_HEAD
        x = jax.random.normal(ks[0], (B, N, D), jnp.float32)
        mask = jax.random.uniform(ks[1], (B, N)) < 0.9
        adjacency_mat = (jax.random.uniform(ks[2], (B, N, N)) < 0.05).astype(jnp.float32)
        distance_mat = jax.random.uniform(ks[3], (B, N, N), jnp.float32) * 5.0
        W_qkv = jax.random.normal(ks[4], (D, inner * 3), jnp.float32) * 0.02
        W_out = jax.random.normal(ks[5], (inner, D), jnp.float32) * 0.02
        b_out = jnp.zeros((D,), jnp.float32)
        return {'x': x, 'mask': mask, 'adjacency_mat': adjacency_mat, 'distance_mat': distance_mat, 'W_qkv': W_qkv, 'W_out': W_out, 'b_out': b_out}
    _L1_gnn_all = _L1_gnn_setup()
    _L1_gnn_in = {k: v for k, v in _L1_gnn_all.items() if k in ('W_qkv', 'W_out', 'b_out')}
    del _L1_gnn_all
    return {'x': x, 'adj': adj, 'nodemask': nodemask, 'L0_gnn_kernel': _L0_gnn_in['kernel'], 'L1_gnn_W_qkv': _L1_gnn_in['W_qkv'], 'L1_gnn_W_out': _L1_gnn_in['W_out'], 'L1_gnn_b_out': _L1_gnn_in['b_out']}

def reference(x, adj, nodemask, L0_gnn_kernel, L1_gnn_W_qkv, L1_gnn_W_out, L1_gnn_b_out):
    import jax
    import jax.numpy as jnp

    def _L0_gnn_ref(x, a, kernel):
        import jax, jax.numpy as jnp
        import numpy as np
        t = jnp.einsum('bnm,bmf->bnf', a, x)
        out = jnp.einsum('bnf,fd->bnd', t, kernel)
        out = jax.nn.relu(out)
        mask = (jnp.sum((x != 0).astype(jnp.float32), axis=-1, keepdims=True) > 0).astype(jnp.float32)
        return out * mask

    def _L1_gnn_ref(x, mask, adjacency_mat, distance_mat, W_qkv, W_out, b_out):
        import jax, jax.numpy as jnp
        import numpy as np
        HEADS = 8
        DIM_HEAD = 64
        LA = 0.33
        LD = 0.33
        LG = 0.33
        B, N, _ = x.shape
        scale = DIM_HEAD ** (-0.5)
        qkv = (x @ W_qkv).reshape(B, N, HEADS, 3, DIM_HEAD)
        q, k, v = (jnp.transpose(qkv[..., i, :], (0, 2, 1, 3)) for i in range(3))
        dots = jnp.einsum('bhid,bhjd->bhij', q, k) * scale
        big = jnp.finfo(dots.dtype).max
        m2 = mask[:, None, :, None] & mask[:, None, None, :]
        dots = jnp.where(m2, dots, -big)
        attn = jax.nn.softmax(dots, axis=-1) * LA
        adj = jnp.where(m2, adjacency_mat[:, None], 0.0)
        dist = jnp.where(m2, distance_mat[:, None], big)
        attn = attn + LG * adj + LD * jnp.exp(-dist)
        out = jnp.einsum('bhij,bhjd->bhid', attn, v)
        out = jnp.transpose(out, (0, 2, 1, 3)).reshape(B, N, HEADS * DIM_HEAD)
        return out @ W_out + b_out
    h = jnp.maximum(_layernorm(x, axis=-1), 0.0)
    x = x + _L0_gnn_ref(h, adj, L0_gnn_kernel)
    h = jnp.maximum(_layernorm(x, axis=-1), 0.0)
    x = x + _L1_gnn_ref(h, nodemask, adj, adj, L1_gnn_W_qkv, L1_gnn_W_out, L1_gnn_b_out)
    return x

_drawn_inputs = setup_inputs


def setup_inputs(seed=0):
    import zlib

    import numpy as np

    out = dict(_drawn_inputs(seed))
    spreads = {'L1_gnn_b_out': (0.0, 0.8)}
    factors = {}
    for name, (base, spread) in spreads.items():
        noise = np.random.default_rng([zlib.crc32(name.encode()), seed]).standard_normal(out[name].shape)
        drawn = base * np.exp(spread * noise) if base else spread * noise
        out[name] = jnp.asarray(drawn.astype(out[name].dtype))
    for name, factor in factors.items():
        out[name] = (out[name] * factor).astype(out[name].dtype)
    return out
```

```python
from contextlib import ExitStack

import concourse.bass as bass
from concourse import mybir

F32 = mybir.dt.float32
F16 = mybir.dt.float16
U8 = mybir.dt.uint8
ALU = mybir.AluOpType
ACT = mybir.ActivationFunctionType
AX_X = mybir.AxisListType.X

P = 128
HEADS = 8
DH = 64
LAMBDA = 0.33
EPS = 1e-5

W_SCALE = 32.0
K_SCALE = 16.0
MASKED = 60000.0
GONE = 1e30

HI, LO = 0, 1
PRODUCTS = ((HI, HI), (HI, LO), (LO, HI))
Q, K, V = 0, 1, 2

F_ADJ, F_T, F_Y, F_H2, F_QK, F_V, F_U, F_USES = 0, 4, 6, 8, 10, 18, 22, 24
M_USES, M_UNITS = 38, 32
O_USES = HEADS + 2


def gnn_kernel(nc, x, adj, nodemask, k0, w_qkv, w_out, b_out, identity, bias_rows, out):
    B, N, D = x.shape
    NT = N // P
    KT = D // P
    PAIRS = HEADS // 2
    HALF = N * NT // 2
    assert (N, D, HEADS * DH) == (512, 256, 512)

    with ExitStack() as ctx:
        def sb(name, shape, dt):
            return ctx.enter_context(nc.sbuf_tensor(name, shape, dt))

        def psum(name, shape):
            return ctx.enter_context(nc.psum_tensor(name, shape, F32))

        def sem(name):
            return ctx.enter_context(nc.semaphore(name))

        ident = sb("ident", [P, P], F32)
        ones = sb("ones", [P, P], F16)
        wqkv = sb("wqkv", [P, 2, KT, 3, N], F16)
        wo = sb("wo", [P, 2, NT, D], F16)
        wk0 = sb("wk0", [P, 2, KT, D], F16)
        wc = sb("wc", [P, 2, KT, D], F16)
        b_bc = sb("b_bc", [P, D], F32)
        par_all = sb("par_all", [P, B, 4, NT], F32)
        par = sb("par", [P, 2, 4, NT], F32)

        xin = sb("xin", [P, NT, D], F32)
        x1 = sb("x1", [P, 2, NT, D], F32)
        adj_sb = sb("adj_sb", [P, NT, N], F32)
        adjT = sb("adjT", [P, 2, NT, N], F16)
        e_sb = sb("e_sb", [P, 2, N], F32)
        gT = sb("gT", [P, 2, NT, N], F16)
        h_f = sb("h_f", [P, NT, D], F32)
        h_s = sb("h_s", [P, 2, NT, D], F16)
        hT = sb("hT", [P, 2, KT, N], F16)
        uT = sb("uT", [P, 2, KT, N], F16)
        slab = sb("slab", [P, 2, 2, 2, N], F16)
        qm = sb("qm", [P, 4, N], F16)
        stats = sb("stats", [P, NT, 6], F32)
        meanvar = sb("meanvar", [P, NT, 2], F32)
        var_eps = sb("var_eps", [P, NT], F32)
        minus_half = sb("minus_half", [P, NT], F32)
        rstd = sb("rstd", [P, NT], F32)
        nbias = sb("nbias", [P, NT], F32)
        h_sum = sb("h_sum", [P, NT], F32)
        row_used = sb("row_used", [P, NT], F32)
        f_sum = sb("f_sum", [P, KT], F32)
        mean_rep = sb("mean_rep", [P, 2, KT, P], F16)
        maxima = sb("maxima", [P, NT, HEADS], F32)
        m_row = sb("m_row", [HEADS, N], F16)

        ka = sb("ka", [P, 2, HEADS, N], F16)
        qa = sb("qa", [P, 2, HEADS, N], F16)
        km = sb("km", [P, 2, HEADS, N], F16)
        qb = sb("qb", [P, 2, HEADS, N], F16)
        vh = sb("vh", [P, 2, NT, HEADS, DH + 2], F16)
        vl = sb("vl", [P, 2, NT, HEADS, DH], F16)
        p_f = sb("p_f", [P, 2, HALF], F32)
        p_s = sb("p_s", [P, 2, 2, 2, HALF], F16)
        recip = sb("recip", [P, NT], F32)
        o_pair = sb("o_pair", [P, NT, P], F32)
        oT = sb("oT", [P, 2, PAIRS, N], F16)

        raw_qkv = p_s[:].rearrange("p a b c n -> p (a b c n)").bitcast(F32)[:, 0:KT * 3 * N].rearrange(
            "p (k n) -> p k n", k=KT)
        raw_out = p_f[:, 0, :].rearrange("p (t n) -> p t n", t=NT)
        raw_k0 = p_f[:, 1, 0:KT * D].rearrange("p (t n) -> p t n", t=KT)
        raw_v = x1[:, 1].rearrange("p t n -> p (t n)").rearrange("p (k n) -> p k n", k=KT)
        wvT = gT[:].rearrange("p a t n -> p (a t n)").bitcast(F32)[:, 0:NT * D].rearrange(
            "p (t n) -> p t n", t=NT)

        mask_f = e_sb[0:B * NT, 0, 0:P]
        mask_bias = e_sb[0:B * NT, 1, 0:P // 2].bitcast(F16)
        mask_rows = e_sb[0:B * NT, 1, P:P + P // 4].bitcast(U8)

        s_ps = psum("s_ps", [P, 2, 2, N])
        f_ps = psum("f_ps", [P, 2, N])
        m_ps = psum("m_ps", [P, N])
        o_ps = psum("o_ps", [P, N])

        raw_loaded = [sem(f"raw_loaded{i}") for i in range(5)]
        setup_dve = sem("setup_dve")
        setup_act = sem("setup_act")
        setup_pe = sem("setup_pe")
        bias_stored = sem("bias_stored")
        x_loaded = sem("x_loaded")
        adj_loaded = sem("adj_loaded")
        par_ready = sem("par_ready")
        ln_stats = sem("ln_stats")
        ln_aggr = sem("ln_aggr")
        ln_var = sem("ln_var")
        ln_rstd = sem("ln_rstd")
        ln_bias = sem("ln_bias")
        ln_relu = sem("ln_relu")
        row_used_ready = sem("row_used_ready")
        h_hi = sem("h_hi")
        h_lo = sem("h_lo")
        f_full = sem("f_full")
        f_hi = sem("f_hi")
        f_free = [sem("f_free0"), sem("f_free1")]
        g_hi = sem("g_hi")
        g_lo = sem("g_lo")
        y_added = sem("y_added")
        b_added = sem("b_added")
        mean_hi = sem("mean_hi")
        mean_ready = sem("mean_ready")
        moved = [sem("moved0"), sem("moved1")]
        qm_moved = [sem("qm_moved0"), sem("qm_moved1")]
        bias_moved = sem("bias_moved")
        max_moved = sem("max_moved")
        m_full = sem("m_full")
        m_hi = sem("m_hi")
        m_free = sem("m_free")
        s_full = sem("s_full")
        exp_done = sem("exp_done")
        p_hi = sem("p_hi")
        p_lo = [sem("p_lo0"), sem("p_lo1")]
        o_full = sem("o_full")
        o_free = sem("o_free")
        recip_done = sem("recip_done")
        stored = sem("stored")

        def wait(eng, s, value):
            if not (isinstance(value, int) and value <= 0):
                eng.wait_ge(s, value)

        def m_pair(b, t):
            if isinstance(b, int) and b == B - 1:
                return 34 + M_USES * b + t
            return 33 + M_USES * b + (1, 3, 20, M_USES)[t]

        def m_blend(f):
            return 0 if isinstance(f, int) and f == 0 else 33 + M_USES * (f - 1) + 2

        def m_unit(f, u):
            if isinstance(f, int) and f == 0:
                return 1 + u
            return 33 + M_USES * (f - 1) + (4 + u if u < M_UNITS // 2 else 5 + u)

        def m_max(f):
            return 33 if isinstance(f, int) and f == 0 else 33 + M_USES * (f - 1) + M_USES - 1

        def f_count(f, i):
            return F_USES // 2 * f + i // 2 + 1

        def hi_count(f, i):
            return (F_USES - 2) * f + (i if i < F_Y else i - 2) + 1

        LOOP = (1, B - 3)

        def entries(eng, body, first):
            first()
            body(0, 0)
            with eng.Fori(0, (LOOP[1] - LOOP[0]) // 2) as turn:
                for k in range(2):
                    body(turn * 2 + (1 + k), (1 + k) % 2)
            for b in range(LOOP[1], B):
                body(b, b % 2)

        def has_front(b):
            return not (isinstance(b, int) and b + 1 >= B)

        def has_load(b):
            return not (isinstance(b, int) and b + 2 >= B)

        def after_first(b):
            return not (isinstance(b, int) and b == 0)

        ctx.enter_context(nc.allow_non_contiguous_dma(reason="mask rows and head placement"))
        block = ctx.enter_context(nc.Block())

        @block.sync
        def _(sp):
            def load_x(f):
                wait(sp, y_added, 2 * f)
                sp.dma_start(xin[:], x[f].rearrange("(t p) f -> p t f", p=P)).then_inc(x_loaded, 16)

            def load_adj(f):
                wait(sp, f_full, F_USES * (f - 1) + F_T)
                sp.dma_start(adj_sb[:], adj[f].rearrange("(t p) m -> p t m", p=P)).then_inc(adj_loaded, 16)

            def move_mask_bias(f, p):
                wait(sp, f_full, F_USES * f + F_QK + 1)
                row = bias_rows[f].unsqueeze(0).unsqueeze(0)
                sp.dma_start(km[DH:DH + 1, p, :, :], row.to_broadcast([1, HEADS, N])).then_inc(bias_moved, 16)

            def move_heads(f, p, g):
                sp.wait_ge(f_free[0], f_count(f, F_QK + 4 * g + 2))
                sp.wait_ge(f_free[1], f_count(f, F_QK + 4 * g + 3))
                for odd in range(2):
                    src = slice(DH * odd, DH * odd + DH)
                    dst = slice(4 * g + odd, 4 * g + 4, 2)
                    for tile, rows, which, part in (
                        (ka, 0, K, HI), (ka, DH, K, LO), (km, 0, K, HI),
                        (qa, 0, Q, HI), (qa, DH, Q, HI), (qb, 0, Q, LO),
                    ):
                        sp.dma_start(tile[rows:rows + DH, p, dst, :],
                                     slab[src, which, part, :, :]).then_inc(moved[g], 16)
                if g == 1:
                    sp.wait_ge(m_full, m_unit(f, M_UNITS // 2 - 1) + 1)
                for odd in range(2):
                    src = slice(DH * odd, DH * odd + DH)
                    sp.dma_start(qm[0:DH, odd:4:2, :], slab[src, Q, HI, :, :]).then_inc(qm_moved[g], 16)

            def move_maxima(f, p):
                sp.wait_ge(m_free, m_max(f) + 1)
                sp.dma_start(qb[DH + 1:DH + 2, p, :, :], m_row[:, :]).then_inc(max_moved, 16)

            def store(b, p):
                sp.wait_ge(o_free, O_USES * (b + 1))
                sp.dma_start(out[b].rearrange("(t p) f -> p t f", p=P), x1[:, p]).then_inc(stored, 16)

            def first():
                sp.dma_start(ident[:], identity).then_inc(raw_loaded[0], 16)
                sp.dma_start(mask_rows, nodemask.rearrange("b (t p) -> (b t) p", p=P)).then_inc(raw_loaded[0], 16)
                sp.dma_start(raw_qkv, w_qkv.rearrange("(k p) n -> p k n", p=P)).then_inc(raw_loaded[1], 16)
                sp.dma_start(raw_out, w_out.rearrange("(t p) n -> p t n", p=P)).then_inc(raw_loaded[2], 16)
                sp.dma_start(raw_k0, k0.rearrange("(t p) n -> p t n", p=P)).then_inc(raw_loaded[3], 16)
                load_x(0)
                load_adj(0)
                sp.dma_start(b_bc[:], b_out.unsqueeze(0).to_broadcast([P, D])).then_inc(raw_loaded[4], 16)
                sp.wait_ge(setup_dve, 2)
                sp.dma_start(bias_rows.rearrange("b (t p) -> (b t) p", p=P), mask_bias).then_inc(bias_stored, 16)
                sp.wait_ge(bias_stored, 16)
                load_adj(1)
                load_x(1)
                move_mask_bias(0, 0)
                move_heads(0, 0, 0)
                move_heads(0, 0, 1)
                move_maxima(0, 0)

            def body(b, p):
                if after_first(b):
                    store(b - 1, 1 - p)
                if has_load(b):
                    load_adj(b + 2)
                    load_x(b + 2)
                if has_front(b):
                    move_mask_bias(b + 1, 1 - p)
                    move_heads(b + 1, 1 - p, 0)
                    move_heads(b + 1, 1 - p, 1)
                    move_maxima(b + 1, 1 - p)

            entries(sp, body, first)
            store(B - 1, (B - 1) % 2)
            sp.wait_ge(stored, 16 * B)

        @block.tensor
        def _(pe):
            def split_mm(dst, lhs, rhs, tiles, open_group=True, close_group=True):
                steps = [(i, a, c) for i in range(tiles) for a, c in PRODUCTS]
                for n, (i, a, c) in enumerate(steps):
                    last = nc.tensor.matmul(dst, lhs(a, i), rhs(c, i), start=open_group and n == 0,
                                            stop=close_group and n == len(steps) - 1)
                return last

            def f_bank(f, i):
                wait(pe, f_free[i % 2], F_USES // 2 * f + i // 2)
                return f_ps[:, i % 2, :]

            def both_evacuated(f, i):
                pe.wait_ge(f_free[0], f_count(f, i - 1))
                pe.wait_ge(f_free[1], f_count(f, i))

            def adj_transposes(f):
                pe.wait_ge(adj_loaded, 16 * (f + 1))
                for jt in range(NT):
                    bank = f_bank(f, F_ADJ + jt)
                    for it in range(NT):
                        last = nc.tensor.transpose(bank[:, it * P:(it + 1) * P],
                                                   adj_sb[:, it, jt * P:(jt + 1) * P], ident[:])
                    last.then_inc(f_full, 1)

            def adj_h1(f):
                both_evacuated(f, F_T - 1)
                pe.wait_ge(h_lo, 2 * f + 1)
                for ft in range(KT):
                    bank = f_bank(f, F_T + ft)
                    split_mm(bank, lambda a, i: h_s[:, a, i, ft * P:(ft + 1) * P],
                             lambda c, i: adjT[:, c, i, :], NT).then_inc(f_full, 1)

            def t_kernel(f):
                both_evacuated(f, F_Y - 1)
                for half in range(2):
                    bank = f_bank(f, F_Y + half)
                    for k in range(2):
                        it = 2 * half + k
                        last = split_mm(bank[:, k * D:(k + 1) * D],
                                        lambda a, i: hT[:, a, i, it * P:(it + 1) * P],
                                        lambda c, i: wk0[:, c, i, :], KT)
                    last.then_inc(f_full, 1)

            def h2_transposes(f):
                pe.wait_ge(ln_relu, 2 * f + 2)
                for ft in range(KT):
                    bank = f_bank(f, F_H2 + ft)
                    for it in range(NT):
                        last = nc.tensor.transpose(bank[:, it * P:(it + 1) * P],
                                                   h_f[:, it, ft * P:(ft + 1) * P], ident[:])
                    last.then_inc(f_full, 1)

            def queries_keys(f, pair):
                if pair == 0:
                    both_evacuated(f, F_QK - 1)
                for which in (Q, K):
                    bank = f_bank(f, F_QK + 2 * pair + which)
                    split_mm(bank, lambda a, i: wqkv[:, a, i, which, pair * P:(pair + 1) * P],
                             lambda c, i: hT[:, c, i, :], KT).then_inc(f_full, 1)

            def values(f):
                for jt in range(NT):
                    bank = f_bank(f, F_V + jt)
                    split_mm(bank, lambda a, i: hT[:, a, i, jt * P:(jt + 1) * P],
                             lambda c, i: wqkv[:, c, i, V, :], KT).then_inc(f_full, 1)

            def u_product(f):
                pe.wait_ge(g_lo, NT * (f + 1))
                pe.wait_ge(h_lo, 2 * f + 2)
                for ft in range(KT):
                    bank = f_bank(f, F_U + ft)
                    split_mm(bank, lambda a, i: h_s[:, a, i, ft * P:(ft + 1) * P],
                             lambda c, i: gT[:, c, i, :], NT).then_inc(f_full, 1)

            def blend_row(f):
                pe.wait_ge(mean_ready, f + 1)
                wait(pe, m_free, m_blend(f))
                split_mm(m_ps[:, 0:D], lambda a, i: mean_rep[:, a, i, :],
                         lambda c, i: wc[:, c, i, :], KT).then_inc(m_full, 1)

            def maxima_unit(f, p, u):
                h, it = u // NT, u % NT
                if u == 0:
                    pe.wait_ge(bias_moved, 16 * (f + 1))
                if u % (M_UNITS // 2) == 0:
                    g = u // (M_UNITS // 2)
                    pe.wait_ge(moved[g], 12 * 16 * (f + 1))
                    pe.wait_ge(qm_moved[g], 2 * 16 * (f + 1))
                wait(pe, m_free, m_unit(f, u))
                nc.tensor.matmul(m_ps[:], qm[0:DH + 1, h % 4, it * P:(it + 1) * P],
                                 km[0:DH + 1, p, h, :], start=True, stop=True).then_inc(m_full, 1)

            def maxima_transpose(f):
                wait(pe, m_free, m_max(f))
                for it in range(NT):
                    last = nc.tensor.transpose(m_ps[0:HEADS, it * P:(it + 1) * P], maxima[:, it, :], ident[:])
                last.then_inc(m_full, 1)

            def scores(b, p, h):
                if h == 0:
                    pe.wait_ge(max_moved, 16 * (b + 1))
                for half in range(2):
                    wait(pe, exp_done, 2 * (HEADS * b + h) + half - 1)
                    for k in range(2):
                        cols = slice((2 * half + k) * P, (2 * half + k + 1) * P)
                        nc.tensor.matmul(s_ps[:, half, k, :], ka[:, p, h, cols], qa[:, p, h, :],
                                         start=True, stop=False)
                        last = nc.tensor.matmul(s_ps[:, half, k, :], km[0:DH + 2, p, h, cols],
                                                qb[0:DH + 2, p, h, :], start=False, stop=True)
                    last.then_inc(s_full, 1)

            def attend(b, p, h):
                if h == 0:
                    both_evacuated(b, F_V + NT - 1)
                wait(pe, o_free, O_USES * b + h)
                for half in range(2):
                    pe.wait_ge(p_lo[half], HEADS * b + h + 1)
                    for k in range(2):
                        jt = 2 * half + k
                        for it in range(NT):
                            dst = o_ps[:, it * (DH + 1):(it + 1) * (DH + 1)]
                            cols = slice(k * N + it * P, k * N + (it + 1) * P)
                            hi = p_s[:, h % 2, half, HI, cols]
                            lo = p_s[:, h % 2, half, LO, cols]
                            nc.tensor.matmul(dst, hi, vh[:, p, jt, h, 0:DH + 1],
                                             start=jt == 0 and it == 0, stop=False, skip_group_check=True)
                            nc.tensor.matmul(dst[:, 0:DH], hi, vl[:, p, jt, h, :],
                                             start=False, stop=False, skip_group_check=True)
                            last = nc.tensor.matmul(dst, lo, vh[:, p, jt, h, 0:DH + 1],
                                                    start=False, stop=jt == NT - 1, skip_group_check=True)
                last.then_inc(o_full, 1)

            def pair_transposes(b, t):
                pe.wait_ge(o_free, O_USES * b + 2 * t + 2)
                wait(pe, m_free, m_pair(b, t))
                for it in range(NT):
                    last = nc.tensor.transpose(m_ps[:, it * P:(it + 1) * P], o_pair[:, it, :], ident[:])
                last.then_inc(m_full, 1)

            def projection(b, half):
                pe.wait_ge(o_free, O_USES * b + HEADS + half)
                if half == 0:
                    both_evacuated(b, F_U + 1)
                    pe.wait_ge(m_free, m_pair(b, PAIRS - 1) + 1)
                for k in range(2):
                    it = 2 * half + k
                    rows = slice(it * P, (it + 1) * P)
                    dst = o_ps[:, k * D:(k + 1) * D]
                    split_mm(dst, lambda a, i: uT[:, a, i, rows], lambda c, i: wc[:, c, i, :], KT,
                             close_group=False)
                    last = split_mm(dst, lambda a, i: oT[:, a, i, rows], lambda c, i: wo[:, c, i, :],
                                    PAIRS, open_group=False)
                last.then_inc(o_full, 1)

            def first():
                pe.wait_ge(raw_loaded[0], 32)
                pe.wait_ge(setup_dve, 1)
                nc.tensor.transpose(m_ps[:, 0:B * NT], mask_f, ident[0:B * NT, 0:B * NT]).then_inc(setup_pe, 1)
                pe.wait_ge(setup_act, 1)
                for t in range(NT):
                    for kt in range(KT):
                        last = nc.tensor.transpose(
                            f_ps[:, t // 2, (t % 2) * D + kt * P:(t % 2) * D + (kt + 1) * P],
                            raw_v[:, kt, t * P:(t + 1) * P], ident[:])
                last.then_inc(setup_pe, 1)
                pe.wait_ge(setup_act, 2)
                pe.wait_ge(setup_dve, 3)
                for kt in range(KT):
                    for t in range(NT):
                        last = nc.tensor.matmul(o_ps[:, kt * D:(kt + 1) * D], wvT[:, t, kt * P:(kt + 1) * P],
                                                raw_out[:, t, :], start=t == 0, stop=t == NT - 1)
                last.then_inc(setup_pe, 1)
                pe.wait_ge(setup_dve, 5)
                adj_transposes(0)
                adj_h1(0)
                t_kernel(0)
                h2_transposes(0)
                blend_row(0)
                for pair in range(PAIRS):
                    queries_keys(0, pair)
                for u in range(M_UNITS):
                    maxima_unit(0, 0, u)
                maxima_transpose(0)

            def body(b, p):
                f, q = b + 1, 1 - p
                front = has_front(b)
                values(b)
                scores(b, p, 0)
                if after_first(b):
                    attend(b - 1, q, HEADS - 1)
                scores(b, p, 1)
                if after_first(b):
                    pair_transposes(b - 1, PAIRS - 1)
                    projection(b - 1, 0)
                    projection(b - 1, 1)
                u_product(b)
                attend(b, p, 0)
                scores(b, p, 2)
                if front:
                    adj_transposes(f)
                    adj_h1(f)
                attend(b, p, 1)
                scores(b, p, 3)
                pair_transposes(b, 0)
                if front:
                    t_kernel(f)
                attend(b, p, 2)
                scores(b, p, 4)
                attend(b, p, 3)
                if front:
                    h2_transposes(f)
                    blend_row(f)
                    queries_keys(f, 0)
                    queries_keys(f, 1)
                scores(b, p, 5)
                pair_transposes(b, 1)
                if front:
                    queries_keys(f, 2)
                    queries_keys(f, 3)
                attend(b, p, 4)
                scores(b, p, 6)
                if front:
                    for u in range(M_UNITS // 2):
                        maxima_unit(f, q, u)
                attend(b, p, 5)
                scores(b, p, 7)
                pair_transposes(b, 2)
                if front:
                    for u in range(M_UNITS // 2, M_UNITS):
                        maxima_unit(f, q, u)
                    maxima_transpose(f)
                attend(b, p, 6)

            entries(pe, body, first)
            attend(B - 1, (B - 1) % 2, HEADS - 1)
            pair_transposes(B - 1, PAIRS - 1)
            projection(B - 1, 0)
            projection(B - 1, 1)

        @block.scalar
        def _(act):
            def relu_norm(f, p, layer):
                act.wait_ge(ln_bias, 2 * f + layer + 1)
                src = xin if layer == 0 else x1[:, p]
                if layer == 0:
                    wait(act, f_full, F_USES * (f - 1) + F_QK)
                    wait(act, h_lo, 2 * f)
                for t in range(NT):
                    last = nc.scalar.activation(h_f[:, t, :], src[:, t, :], ACT.Relu, bias=nbias[:, t:t + 1],
                                                scale=rstd[:, t:t + 1],
                                                accum_out=h_sum[:, t:t + 1] if layer == 0 else None)
                last.then_inc(ln_relu, 1)

            def split_hi(f, i, dst, scale=1.0, **more):
                act.wait_ge(f_full, F_USES * f + i + 1)
                nc.scalar.activation(dst, f_ps[:, i % 2, :], ACT.Copy, scale=scale, **more).then_inc(f_hi, 1)

            def adj_parts(f, p):
                act.wait_ge(par_ready, f + 1)
                for jt in range(NT):
                    i = F_ADJ + jt
                    act.wait_ge(f_full, F_USES * f + i + 1)
                    nc.scalar.activation(adjT[:, HI, jt, :], f_ps[:, i % 2, :], ACT.Copy)
                    wait(act, g_lo, NT * f + jt - 1)
                    nc.scalar.activation(e_sb[:, jt % 2, :], f_ps[:, i % 2, :], ACT.Exp, scale=-1.0,
                                         bias=par[:, p, 1, jt:jt + 1]).then_inc(f_hi, 1)

            def relu_y(f):
                act.wait_ge(row_used_ready, f + 1)
                for half in range(2):
                    i = F_Y + half
                    act.wait_ge(f_full, F_USES * f + i + 1)
                    for k in range(2):
                        it = 2 * half + k
                        last = nc.scalar.activation(h_f[:, it, :], f_ps[:, i % 2, k * D:(k + 1) * D], ACT.Relu,
                                                    scale=row_used[:, it:it + 1])
                    last.then_inc(f_free[i % 2], 1)

            def hi_h2T(f):
                for ft in range(KT):
                    split_hi(f, F_H2 + ft, hT[:, HI, ft, :], accum_out=f_sum[:, ft:ft + 1])

            def hi_pair(f, pair):
                if pair == 0:
                    wait(act, moved[1], 12 * 16 * f)
                    wait(act, qm_moved[1], 2 * 16 * f)
                if pair == 2:
                    act.wait_ge(moved[0], 12 * 16 * (f + 1))
                    act.wait_ge(qm_moved[0], 2 * 16 * (f + 1))
                for which in (Q, K):
                    split_hi(f, F_QK + 2 * pair + which, slab[:, which, HI, pair % 2, :], scale=1 / W_SCALE)

            def hi_values(f, p):
                for jt in range(NT):
                    i = F_V + jt
                    act.wait_ge(f_full, F_USES * f + i + 1)
                    nc.scalar.activation(vh[:, p, jt, :, 0:DH],
                                         f_ps[:, i % 2, :].rearrange("p (h d) -> p h d", d=DH),
                                         ACT.Copy, scale=1 / W_SCALE).then_inc(f_hi, 1)

            def hi_u(f):
                for ft in range(KT):
                    split_hi(f, F_U + ft, uT[:, HI, ft, :])

            def negate_maxima(f):
                act.wait_ge(m_full, m_max(f) + 1)
                wait(act, max_moved, 16 * f)
                nc.scalar.activation(m_row[:, :], m_ps[0:HEADS, :], ACT.Copy, scale=-1.0).then_inc(m_free, 1)

            def exponentials(b, h):
                for half in range(2):
                    act.wait_ge(s_full, 2 * (HEADS * b + h) + half + 1)
                    wait(act, p_lo[half], HEADS * b + h)
                    nc.scalar.activation(p_f[:, half, :].rearrange("p (k n) -> p k n", k=2), s_ps[:, half],
                                         ACT.Exp, scale=DH ** -0.5).then_inc(exp_done, 1)

            def hi_pair_out(b, t):
                act.wait_ge(m_full, m_pair(b, t) + 1)
                nc.scalar.activation(oT[:, HI, t, :], m_ps[:], ACT.Copy).then_inc(m_hi, 1)

            def first():
                act.wait_ge(raw_loaded[1], 16)
                for kt in range(KT):
                    src = raw_qkv[:, kt, :].rearrange("p (h three d) -> p h three d", three=3, d=DH)
                    nc.scalar.activation(raw_v[:, kt, :].rearrange("p (h d) -> p h d", d=DH), src[:, :, V, :],
                                         ACT.Copy)
                    for which in (Q, K, V):
                        src = raw_qkv[:, kt, :].rearrange("p (h three d) -> p h three d", three=3, d=DH)
                        last = nc.scalar.activation(
                            wqkv[:, HI, kt, which, :].rearrange("p (h d) -> p h d", d=DH),
                            src[:, :, which, :], ACT.Copy, scale=W_SCALE)
                last.then_inc(setup_act, 1)
                act.wait_ge(setup_pe, 2)
                for k in range(2):
                    last = nc.scalar.activation(
                        wvT[:, 2 * k:2 * k + 2, :],
                        f_ps[:, k, :].rearrange("p (t n) -> p t n", t=2), ACT.Copy)
                last.then_inc(setup_act, 1)
                act.wait_ge(setup_pe, 3)
                nc.scalar.activation(wc[:, HI], o_ps[:].rearrange("p (k n) -> p k n", k=KT),
                                     ACT.Copy).then_inc(setup_act, 1)
                relu_norm(0, 0, 0)
                act.wait_ge(bias_stored, 16)
                adj_parts(0, 0)
                for ft in range(KT):
                    split_hi(0, F_T + ft, hT[:, HI, ft, :])
                relu_y(0)
                relu_norm(0, 0, 1)
                hi_h2T(0)
                for pair in range(PAIRS):
                    hi_pair(0, pair)
                negate_maxima(0)

            def body(b, p):
                f, q = b + 1, 1 - p
                front = has_front(b)
                hi_values(b, p)
                exponentials(b, 0)
                if front:
                    relu_norm(f, q, 0)
                exponentials(b, 1)
                if after_first(b):
                    hi_pair_out(b - 1, PAIRS - 1)
                hi_u(b)
                exponentials(b, 2)
                if front:
                    adj_parts(f, q)
                    for ft in range(KT):
                        split_hi(f, F_T + ft, hT[:, HI, ft, :])
                exponentials(b, 3)
                hi_pair_out(b, 0)
                if front:
                    relu_y(f)
                exponentials(b, 4)
                if front:
                    relu_norm(f, q, 1)
                    hi_h2T(f)
                    hi_pair(f, 0)
                    hi_pair(f, 1)
                exponentials(b, 5)
                hi_pair_out(b, 1)
                if front:
                    hi_pair(f, 2)
                    hi_pair(f, 3)
                exponentials(b, 6)
                exponentials(b, 7)
                hi_pair_out(b, 2)
                if front:
                    negate_maxima(f)

            entries(act, body, first)
            hi_pair_out(B - 1, PAIRS - 1)

        @block.vector
        def _(dve):
            def norm_stats(f, p, layer):
                k = 2 * f + layer + 1
                if layer == 0:
                    dve.wait_ge(x_loaded, 16 * (f + 1))
                else:
                    dve.wait_ge(y_added, 2 * (f + 1))
                src = xin if layer == 0 else x1[:, p]
                for t in range(NT):
                    last = nc.vector.bn_stats(stats[:, t, :], src[:, t, :])
                last.then_inc(ln_stats, 1)
                dve.wait_ge(ln_stats, k)
                nc.vector.memset(var_eps[:], EPS)
                for t in range(NT):
                    last = nc.vector.bn_aggr(meanvar[:, t, :], stats[:, t, :])
                last.then_inc(ln_aggr, 1)
                dve.wait_ge(ln_aggr, k)
                nc.vector.tensor_tensor(var_eps[:], meanvar[:, :, 1], var_eps[:], ALU.add).then_inc(ln_var, 1)

            def norm_bias(f, layer):
                dve.wait_ge(ln_rstd, 2 * f + layer + 1)
                nc.vector.scalar_tensor_tensor(nbias[:], meanvar[:, :, 0], -1.0, rstd[:], ALU.mult,
                                               ALU.mult).then_inc(ln_bias, 1)

            def h_high(f, layer):
                dve.wait_ge(ln_relu, 2 * f + layer + 1)
                if layer == 0:
                    wait(dve, f_full, F_USES * f)
                    nc.vector.tensor_scalar(row_used[:], h_sum[:], 0.0, 1 / K_SCALE, ALU.is_gt,
                                            ALU.mult).then_inc(row_used_ready, 1)
                nc.vector.tensor_copy(h_s[:, HI], h_f[:]).then_inc(h_hi, 1)

            def split_lo(f, i, dst, hi, scale=None):
                dve.wait_ge(f_hi, hi_count(f, i))
                src = f_ps[:, i % 2, :]
                if scale is None:
                    return nc.vector.tensor_tensor(dst, src, hi, ALU.subtract)
                return nc.vector.scalar_tensor_tensor(dst, src, scale, hi, ALU.mult, ALU.subtract)

            def take_par(f, p):
                wait(dve, o_free, O_USES * (f - 1))
                nc.vector.tensor_copy(par[:, p].rearrange("p a t -> p (a t)"),
                                      par_all[:, f].rearrange("p a t -> p (a t)")).then_inc(par_ready, 1)

            def adj_parts(f, p):
                dve.wait_ge(par_ready, f + 1)
                for jt in range(NT):
                    i = F_ADJ + jt
                    split_lo(f, i, adjT[:, LO, jt, :], adjT[:, HI, jt, :])
                    e = e_sb[:, jt % 2, :]
                    nc.vector.scalar_tensor_tensor(e, f_ps[:, i % 2, :], par[:, p, 0, jt:jt + 1], e,
                                                   ALU.mult, ALU.add).then_inc(f_free[i % 2], 1)
                    dve.wait_ge(f_free[i % 2], f_count(f, i))
                    nc.vector.tensor_copy(gT[:, HI, jt, :], e).then_inc(g_hi, 1)

            def lo_t(f):
                for ft in range(KT):
                    i = F_T + ft
                    split_lo(f, i, hT[:, LO, ft, :], hT[:, HI, ft, :]).then_inc(f_free[i % 2], 1)

            def add_y(f, p):
                wait(dve, stored, 16 * (f - 1))
                for half in range(2):
                    dve.wait_ge(f_free[half], f_count(f, F_Y + half))
                    rows = slice(2 * half, 2 * half + 2)
                    nc.vector.tensor_tensor(x1[:, p, rows, :], xin[:, rows, :], h_f[:, rows, :],
                                            ALU.add).then_inc(y_added, 1)

            def lo_h2T(f):
                for ft in range(KT):
                    i = F_H2 + ft
                    split_lo(f, i, hT[:, LO, ft, :], hT[:, HI, ft, :]).then_inc(f_free[i % 2], 1)
                for ft in range(KT):
                    last = nc.vector.tensor_scalar(mean_rep[:, HI, ft, :], ones[:], f_sum[:, ft:ft + 1], None,
                                                   ALU.mult)
                last.then_inc(mean_hi, 1)
                dve.wait_ge(mean_hi, f + 1)
                for ft in range(KT):
                    last = nc.vector.scalar_tensor_tensor(mean_rep[:, LO, ft, :], ones[:], f_sum[:, ft:ft + 1],
                                                          mean_rep[:, HI, ft, :], ALU.mult, ALU.subtract)
                last.then_inc(mean_ready, 1)

            def add_blend(f, p):
                dve.wait_ge(m_full, m_blend(f) + 1)
                dve.wait_ge(b_added, f + 1)
                for it in range(NT):
                    last = nc.vector.scalar_tensor_tensor(x1[:, p, it, :], m_ps[:, 0:D], par[:, p, 3, it:it + 1],
                                                          x1[:, p, it, :], ALU.mult, ALU.add)
                last.then_inc(m_free, 1)

            def lo_pair(f, pair):
                for which in (Q, K):
                    i = F_QK + 2 * pair + which
                    split_lo(f, i, slab[:, which, LO, pair % 2, :], slab[:, which, HI, pair % 2, :],
                             1 / W_SCALE).then_inc(f_free[i % 2], 1)

            def lo_values(f, p):
                for jt in range(NT):
                    i = F_V + jt
                    dve.wait_ge(f_hi, hi_count(f, i))
                    nc.vector.scalar_tensor_tensor(
                        vl[:, p, jt], f_ps[:, i % 2, :].rearrange("p (h d) -> p h d", d=DH), 1 / W_SCALE,
                        vh[:, p, jt, :, 0:DH], ALU.mult, ALU.subtract).then_inc(f_free[i % 2], 1)

            def lo_u(f):
                for ft in range(KT):
                    i = F_U + ft
                    split_lo(f, i, uT[:, LO, ft, :], uT[:, HI, ft, :]).then_inc(f_free[i % 2], 1)

            def take_maximum(f, u):
                h, it = u // NT, u % NT
                dve.wait_ge(m_full, m_unit(f, u) + 1)
                nc.vector.reduce_max(maxima[:, it, h:h + 1], m_ps[:], AX_X).then_inc(m_free, 1)

            def split_p(b, h):
                wait(dve, o_full, O_USES * b + h - 1 if h >= 2 else O_USES * (b - 1) + HEADS - 1 + h)
                for half in range(2):
                    dve.wait_ge(exp_done, 2 * (HEADS * b + h) + half + 1)
                    nc.vector.tensor_copy(p_s[:, h % 2, half, HI, :], p_f[:, half, :]).then_inc(p_hi, 1)
                dve.wait_ge(p_hi, 2 * (HEADS * b + h) + 2)
                nc.vector.tensor_tensor(p_s[:, h % 2, 1, LO, :], p_f[:, 1, :], p_s[:, h % 2, 1, HI, :],
                                        ALU.subtract).then_inc(p_lo[1], 1)

            def divide(b, h):
                dve.wait_ge(o_full, O_USES * b + h + 1)
                o = o_ps[:, 0:NT * (DH + 1)].rearrange("p (t d) -> p t d", t=NT)
                nc.vector.reciprocal(recip[:].unsqueeze(2), o[:, :, DH:DH + 1]).then_inc(recip_done, 1)
                dve.wait_ge(recip_done, HEADS * b + h + 1)
                if h % 2 == 0:
                    if h:
                        dve.wait_ge(m_full, m_pair(b, h // 2 - 1) + 1)
                    else:
                        wait(dve, m_full, m_pair(b - 1, PAIRS - 1) + 1 if after_first(b) else 0)
                nc.vector.tensor_tensor(o_pair[:, :, (h % 2) * DH:(h % 2 + 1) * DH], o[:, :, 0:DH],
                                        recip[:].unsqueeze(2).to_broadcast([P, NT, DH]),
                                        ALU.mult).then_inc(o_free, 1)

            def lo_pair_out(b, t):
                dve.wait_ge(m_hi, PAIRS * b + t + 1)
                nc.vector.tensor_tensor(oT[:, LO, t, :], m_ps[:], oT[:, HI, t, :],
                                        ALU.subtract).then_inc(m_free, 1)

            def add_projection(b, p, half):
                dve.wait_ge(o_full, O_USES * b + HEADS + half + 1)
                for k in range(2):
                    it = 2 * half + k
                    last = nc.vector.scalar_tensor_tensor(x1[:, p, it, :], o_ps[:, k * D:(k + 1) * D],
                                                          par[:, p, 2, it:it + 1], x1[:, p, it, :],
                                                          ALU.mult, ALU.add)
                last.then_inc(o_free, 1)

            def first():
                nc.vector.memset(minus_half[:], -0.5)
                nc.vector.memset(km[DH:DH + 2], 1.0)
                nc.vector.memset(qb[DH:DH + 2], 1.0)
                nc.vector.memset(qm[DH:DH + 1], 1.0)
                nc.vector.memset(vh[:, :, :, :, DH:DH + 2], 1.0)
                nc.vector.memset(ones[:], 1.0)
                dve.wait_ge(raw_loaded[0], 32)
                nc.vector.tensor_copy(mask_f, mask_rows).then_inc(setup_dve, 1)
                dve.wait_ge(setup_dve, 1)
                nc.vector.tensor_scalar(mask_bias, mask_f, MASKED, -MASKED, ALU.mult,
                                        ALU.add).then_inc(setup_dve, 1)
                dve.wait_ge(raw_loaded[2], 16)
                nc.vector.tensor_scalar(raw_out, raw_out, LAMBDA * W_SCALE, None, ALU.mult).then_inc(setup_dve, 1)
                dve.wait_ge(setup_pe, 1)
                m = m_ps[:, 0:B * NT].rearrange("p (b t) -> p b t", t=NT)
                for kind, (a, c) in enumerate(((1.0, 0.0), (GONE, -GONE), (1 / W_SCALE, 0.0),
                                               (-1 / (W_SCALE * N), 1 / (W_SCALE * N)))):
                    nc.vector.tensor_scalar(par_all[:, :, kind, :], m, a, c, ALU.mult, ALU.add)
                dve.wait_ge(setup_act, 1)
                for kt in range(KT):
                    for which in (Q, K, V):
                        src = raw_qkv[:, kt, :].rearrange("p (h three d) -> p h three d", three=3, d=DH)
                        nc.vector.scalar_tensor_tensor(
                            wqkv[:, LO, kt, which, :].rearrange("p (h d) -> p h d", d=DH), src[:, :, which, :],
                            W_SCALE, wqkv[:, HI, kt, which, :].rearrange("p (h d) -> p h d", d=DH),
                            ALU.mult, ALU.subtract)
                dve.wait_ge(raw_loaded[3], 16)
                dve.wait_ge(setup_dve, 3)
                nc.vector.tensor_scalar(wk0[:, HI], raw_k0, K_SCALE, None, ALU.mult)
                nc.vector.tensor_copy(wo[:, HI], raw_out).then_inc(setup_dve, 1)
                dve.wait_ge(setup_dve, 4)
                nc.vector.scalar_tensor_tensor(wk0[:, LO], raw_k0, K_SCALE, wk0[:, HI], ALU.mult, ALU.subtract)
                nc.vector.tensor_tensor(wo[:, LO], raw_out, wo[:, HI], ALU.subtract)
                dve.wait_ge(setup_act, 3)
                nc.vector.tensor_tensor(wc[:, LO], o_ps[:].rearrange("p (k n) -> p k n", k=KT), wc[:, HI],
                                        ALU.subtract).then_inc(setup_dve, 1)
                dve.wait_ge(setup_dve, 5)
                take_par(0, 0)
                norm_stats(0, 0, 0)
                norm_bias(0, 0)
                h_high(0, 0)
                adj_parts(0, 0)
                lo_t(0)
                add_y(0, 0)
                norm_stats(0, 0, 1)
                norm_bias(0, 1)
                h_high(0, 1)
                lo_h2T(0)
                add_blend(0, 0)
                for pair in range(PAIRS):
                    lo_pair(0, pair)
                for u in range(M_UNITS):
                    take_maximum(0, u)

            def body(b, p):
                f, q = b + 1, 1 - p
                front = has_front(b)
                lo_values(b, p)
                if front:
                    norm_stats(f, q, 0)
                split_p(b, 0)
                if front:
                    norm_bias(f, 0)
                if after_first(b):
                    divide(b - 1, HEADS - 1)
                split_p(b, 1)
                if after_first(b):
                    lo_pair_out(b - 1, PAIRS - 1)
                    add_projection(b - 1, q, 0)
                    add_projection(b - 1, q, 1)
                lo_u(b)
                if front:
                    take_par(f, q)
                    h_high(f, 0)
                divide(b, 0)
                split_p(b, 2)
                if front:
                    adj_parts(f, q)
                    lo_t(f)
                divide(b, 1)
                split_p(b, 3)
                lo_pair_out(b, 0)
                if front:
                    add_y(f, q)
                    norm_stats(f, q, 1)
                    norm_bias(f, 1)
                divide(b, 2)
                split_p(b, 4)
                divide(b, 3)
                if front:
                    h_high(f, 1)
                    lo_h2T(f)
                    add_blend(f, q)
                    lo_pair(f, 0)
                    lo_pair(f, 1)
                split_p(b, 5)
                lo_pair_out(b, 1)
                if front:
                    lo_pair(f, 2)
                    lo_pair(f, 3)
                divide(b, 4)
                split_p(b, 6)
                if front:
                    for u in range(M_UNITS // 2):
                        take_maximum(f, u)
                divide(b, 5)
                split_p(b, 7)
                lo_pair_out(b, 2)
                if front:
                    for u in range(M_UNITS // 2, M_UNITS):
                        take_maximum(f, u)
                divide(b, 6)

            entries(dve, body, first)
            divide(B - 1, HEADS - 1)
            lo_pair_out(B - 1, PAIRS - 1)
            add_projection(B - 1, (B - 1) % 2, 0)
            add_projection(B - 1, (B - 1) % 2, 1)

        @block.gpsimd
        def _(pool):
            def norm_rstd(f, layer):
                pool.wait_ge(ln_var, 2 * f + layer + 1)
                nc.gpsimd.tensor_tensor(rstd[:], var_eps[:], minus_half[:], ALU.pow).then_inc(ln_rstd, 1)

            def h_low(f, layer):
                pool.wait_ge(h_hi, 2 * f + layer + 1)
                nc.gpsimd.tensor_tensor(h_s[:, LO], h_f[:], h_s[:, HI], ALU.subtract).then_inc(h_lo, 1)

            def g_low(f):
                for jt in range(NT):
                    pool.wait_ge(g_hi, NT * f + jt + 1)
                    nc.gpsimd.tensor_tensor(gT[:, LO, jt, :], e_sb[:, jt % 2, :], gT[:, HI, jt, :],
                                            ALU.subtract).then_inc(g_lo, 1)

            def add_b(f, p):
                pool.wait_ge(ln_relu, 2 * f + 2)
                pool.wait_ge(raw_loaded[4], 16)
                nc.gpsimd.tensor_tensor(x1[:, p], x1[:, p], b_bc[:].unsqueeze(1).to_broadcast([P, NT, D]),
                                        ALU.add).then_inc(b_added, 1)

            def p_low(b, h):
                pool.wait_ge(p_hi, 2 * (HEADS * b + h) + 1)
                nc.gpsimd.tensor_tensor(p_s[:, h % 2, 0, LO, :], p_f[:, 0, :], p_s[:, h % 2, 0, HI, :],
                                        ALU.subtract).then_inc(p_lo[0], 1)

            def first():
                norm_rstd(0, 0)
                h_low(0, 0)
                g_low(0)
                norm_rstd(0, 1)
                h_low(0, 1)
                add_b(0, 0)

            def body(b, p):
                f, q = b + 1, 1 - p
                front = has_front(b)
                if front:
                    norm_rstd(f, 0)
                p_low(b, 0)
                p_low(b, 1)
                if front:
                    h_low(f, 0)
                p_low(b, 2)
                if front:
                    g_low(f)
                p_low(b, 3)
                if front:
                    norm_rstd(f, 1)
                p_low(b, 4)
                if front:
                    h_low(f, 1)
                    add_b(f, q)
                p_low(b, 5)
                p_low(b, 6)
                p_low(b, 7)

            entries(pool, body, first)


_INS = ["x", "adj", "nodemask", "L0_gnn_kernel", "L1_gnn_W_qkv", "L1_gnn_W_out", "L1_gnn_b_out"]


def kernel(**inputs):
    import numpy as _np
    import concourse.bacc as _bacc
    from concourse import mybir as _mybir
    from concourse.bass_utils import run_bass_kernel_spmd as _run

    nc = _bacc.Bacc("TRN2", target_bir_lowering=False, num_devices=1)
    arrays, args = {}, []
    for name in _INS:
        a = _np.ascontiguousarray(inputs[name])
        if a.dtype == _np.bool_:
            a = a.view(_np.uint8)
        arrays[f"in_{name}"] = a
        args.append(nc.dram_tensor(f"in_{name}", a.shape, _mybir.dt.from_np(a.dtype), kind="ExternalInput").ap())
    eye = _np.eye(128, dtype=_np.float32)
    arrays["in_identity"] = eye
    args.append(nc.dram_tensor("in_identity", eye.shape, _mybir.dt.float32, kind="ExternalInput").ap())
    args.append(nc.dram_tensor("mask_bias_rows", inputs["nodemask"].shape, _mybir.dt.float16).ap())
    args.append(nc.dram_tensor("out_0", inputs["x"].shape, _mybir.dt.float32, kind="ExternalOutput").ap())
    gnn_kernel(nc, *args)
    r = _run(nc, [arrays], core_ids=[0])
    return r.results[0]["out_0"]
```

```python
from contextlib import ExitStack

import concourse.bass as bass
from concourse import mybir

F32 = mybir.dt.float32
F16 = mybir.dt.float16
U8 = mybir.dt.uint8
ALU = mybir.AluOpType
ACT = mybir.ActivationFunctionType
AX_X = mybir.AxisListType.X

P = 128
HEADS = 8
DH = 64
LAMBDA = 0.33
EPS = 1e-5

W_SCALE = 32.0
K_SCALE = 16.0
MASKED = 60000.0
GONE = 1e30

POOL_HEADS = (0, 1, 3, 4, 6, 7)

HI, LO = 0, 1
PRODUCTS = ((HI, HI), (HI, LO), (LO, HI))
Q, K, V = 0, 1, 2

F_ADJ, F_T, F_Y, F_H2, F_V, F_U, F_USES = 0, 4, 6, 8, 14, 22, 24
F_PAIR = (10, 12, 18, 20)
S_USES, S_FIRST = 32, 8
M_USES = 7
O_USES = HEADS + 2


def gnn_kernel(nc, x, adj, nodemask, k0, w_qkv, w_out, b_out, identity, bias_rows, out):
    B, N, D = x.shape
    NT = N // P
    KT = D // P
    PAIRS = HEADS // 2
    HALF = N * NT // 2
    assert (N, D, HEADS * DH) == (512, 256, 512)

    with ExitStack() as ctx:
        def sb(name, shape, dt):
            return ctx.enter_context(nc.sbuf_tensor(name, shape, dt))

        def psum(name, shape):
            return ctx.enter_context(nc.psum_tensor(name, shape, F32))

        def sem(name):
            return ctx.enter_context(nc.semaphore(name))

        ident = sb("ident", [P, P], F32)
        ones = sb("ones", [P, P], F16)
        wqkv = sb("wqkv", [P, 2, KT, 3, N], F16)
        wo = sb("wo", [P, 2, NT, D], F16)
        wk0 = sb("wk0", [P, 2, KT, D], F16)
        wc = sb("wc", [P, 2, KT, D], F16)
        b_bc = sb("b_bc", [P, D], F32)
        par_all = sb("par_all", [P, B, 4, NT], F32)
        par = sb("par", [P, 2, 4, NT], F32)

        xin = sb("xin", [P, NT, D], F32)
        x1 = sb("x1", [P, 2, NT, D], F32)
        adj_sb = sb("adj_sb", [P, NT, N], F32)
        adjT = sb("adjT", [P, 2, NT, N], F16)
        e_sb = sb("e_sb", [P, 2, N], F32)
        gT = sb("gT", [P, 2, NT, N], F16)
        h_f = sb("h_f", [P, NT, D], F32)
        h_s = sb("h_s", [P, 2, NT, D], F16)
        hT = sb("hT", [P, 2, KT, N], F16)
        uT = sb("uT", [P, 2, KT, N], F16)
        slab = sb("slab", [P, 2, 2, 2, N], F16)
        qm = sb("qm", [P, 4, N], F16)
        stats = sb("stats", [P, NT, 6], F32)
        meanvar = sb("meanvar", [P, NT, 2], F32)
        var_eps = sb("var_eps", [P, NT], F32)
        minus_half = sb("minus_half", [P, NT], F32)
        rstd = sb("rstd", [P, NT], F32)
        nbias = sb("nbias", [P, NT], F32)
        h_sum = sb("h_sum", [P, NT], F32)
        row_used = sb("row_used", [P, NT], F32)
        f_sum = sb("f_sum", [P, KT], F32)
        mean_rep = sb("mean_rep", [P, 2, KT, P], F16)
        maxima = sb("maxima", [P, HEADS, NT], F32)
        m_row = sb("m_row", [HEADS // 2, N], F16)

        ka = sb("ka", [P, 2, HEADS, N], F16)
        qa = sb("qa", [P, 2, HEADS, N], F16)
        km = sb("km", [P, 2, HEADS, N], F16)
        qb = sb("qb", [P, 2, HEADS, N], F16)
        vh = sb("vh", [P, 2, NT, HEADS, DH + 2], F16)
        vl = sb("vl", [P, 2, NT, HEADS, DH], F16)
        p_f = sb("p_f", [P, 2, HALF], F32)
        p_s = sb("p_s", [P, 2, 2, 2, HALF], F16)
        recip = sb("recip", [P, NT], F32)
        o_pair = sb("o_pair", [P, NT, P], F32)
        oT = sb("oT", [P, 2, PAIRS, N], F16)

        raw_qkv = p_s[:].rearrange("p a b c n -> p (a b c n)").bitcast(F32)[:, 0:KT * 3 * N].rearrange(
            "p (k n) -> p k n", k=KT)
        raw_out = p_f[:, 0, :].rearrange("p (t n) -> p t n", t=NT)
        raw_k0 = p_f[:, 1, 0:KT * D].rearrange("p (t n) -> p t n", t=KT)
        raw_v = x1[:, 1].rearrange("p t n -> p (t n)").rearrange("p (k n) -> p k n", k=KT)
        wvT = gT[:].rearrange("p a t n -> p (a t n)").bitcast(F32)[:, 0:NT * D].rearrange(
            "p (t n) -> p t n", t=NT)

        mask_f = e_sb[0:B * NT, 0, 0:P]
        mask_bias = e_sb[0:B * NT, 1, 0:P // 2].bitcast(F16)
        mask_rows = e_sb[0:B * NT, 1, P:P + P // 4].bitcast(U8)

        s_ps = psum("s_ps", [P, 2, 2, N])
        f_ps = psum("f_ps", [P, 2, N])
        m_ps = psum("m_ps", [P, N])
        o_ps = psum("o_ps", [P, N])

        raw_loaded = [sem(f"raw_loaded{i}") for i in range(5)]
        setup_dve = sem("setup_dve")
        setup_act = sem("setup_act")
        setup_pe = sem("setup_pe")
        bias_stored = sem("bias_stored")
        x_loaded = sem("x_loaded")
        adj_loaded = sem("adj_loaded")
        par_ready = sem("par_ready")
        ln_stats = sem("ln_stats")
        ln_aggr = sem("ln_aggr")
        ln_var = sem("ln_var")
        ln_rstd = sem("ln_rstd")
        ln_bias = sem("ln_bias")
        ln_relu = sem("ln_relu")
        row_used_ready = sem("row_used_ready")
        h_hi = sem("h_hi")
        h_lo = sem("h_lo")
        f_full = sem("f_full")
        f_hi = sem("f_hi")
        f_free = [sem("f_free0"), sem("f_free1")]
        g_hi = sem("g_hi")
        g_lo = sem("g_lo")
        y_added = sem("y_added")
        b_added = sem("b_added")
        mean_hi = sem("mean_hi")
        mean_ready = sem("mean_ready")
        moved = [sem("moved0"), sem("moved1")]
        keys_moved = [sem("keys_moved0"), sem("keys_moved1")]
        bias_moved = sem("bias_moved")
        max_moved = sem("max_moved")
        m_full = sem("m_full")
        m_hi = sem("m_hi")
        m_free = sem("m_free")
        s_full = sem("s_full")
        s_free = [sem("s_free0"), sem("s_free1")]
        p_hi = sem("p_hi")
        p_lo = [sem("p_lo0"), sem("p_lo1")]
        o_full = sem("o_full")
        o_free = sem("o_free")
        recip_done = sem("recip_done")
        stored = sem("stored")

        def wait(eng, s, value):
            if not (isinstance(value, int) and value <= 0):
                eng.wait_ge(s, value)

        def is_last(b):
            return isinstance(b, int) and b == B - 1

        def m_pair(b, t):
            return 1 + M_USES * b + ((0, 2, 3, 4, 5) if is_last(b) else (0, 2, 3, 5, M_USES))[t + 1]

        def m_blend(f):
            return 0 if isinstance(f, int) and f == 0 else 1 + M_USES * (f - 1) + 4

        def m_max(f, g):
            if g == 1:
                return 1 + M_USES * f + 1
            return 1 if isinstance(f, int) and f == 0 else 1 + M_USES * (f - 1) + 6

        def s_score(b, h, half):
            steps = (0, 0, 4, 8, 8, 8, 8, 8 if is_last(b) else 12)[h]
            return S_FIRST + S_USES * b + 2 * h + steps + half

        def s_max(f, g, j):
            if g == 1:
                return S_FIRST + S_USES * f + (4 + j if j < 4 else 6 + j)
            if isinstance(f, int) and f == 0:
                return j
            return S_FIRST + S_USES * (f - 1) + (22 + j if j < 4 else 24 + j)

        def s_before(use, half):
            return (use - half) // 2

        def f_count(f, i):
            return F_USES // 2 * f + i // 2 + 1

        def hi_count(f, i):
            return (F_USES - 2) * f + (i if i < F_Y else i - 2) + 1

        LOOP = (1, B - 3)

        def entries(eng, body, first):
            first()
            body(0, 0)
            with eng.Fori(0, (LOOP[1] - LOOP[0]) // 2) as turn:
                for k in range(2):
                    body(turn * 2 + (1 + k), (1 + k) % 2)
            for b in range(LOOP[1], B):
                body(b, b % 2)

        def has_front(b):
            return not (isinstance(b, int) and b + 1 >= B)

        def has_load(b):
            return not (isinstance(b, int) and b + 2 >= B)

        def after_first(b):
            return not (isinstance(b, int) and b == 0)

        ctx.enter_context(nc.allow_non_contiguous_dma(reason="mask rows and head placement"))
        block = ctx.enter_context(nc.Block())

        @block.sync
        def _(sp):
            def load_x(f):
                wait(sp, y_added, 2 * f)
                sp.dma_start(xin[:], x[f].rearrange("(t p) f -> p t f", p=P)).then_inc(x_loaded, 16)

            def load_adj(f):
                wait(sp, f_full, F_USES * (f - 1) + F_T)
                sp.dma_start(adj_sb[:], adj[f].rearrange("(t p) m -> p t m", p=P)).then_inc(adj_loaded, 16)

            def move_mask_bias(f, p):
                wait(sp, f_full, F_USES * f + F_PAIR[0] + 1)
                row = bias_rows[f].unsqueeze(0).unsqueeze(0)
                sp.dma_start(km[DH:DH + 1, p, :, :], row.to_broadcast([1, HEADS, N])).then_inc(bias_moved, 16)

            def move_heads(f, p, g):
                sp.wait_ge(f_free[0], f_count(f, F_PAIR[2 * g + 1]))
                sp.wait_ge(f_free[1], f_count(f, F_PAIR[2 * g + 1] + 1))
                if g == 1:
                    sp.wait_ge(s_full, s_max(f, 0, 7) + 1)
                for tile, rows, which, part, done in (
                    (km, 0, K, HI, keys_moved), (qm, 0, Q, HI, keys_moved),
                    (qa, 0, Q, HI, moved), (qa, DH, Q, HI, moved), (qb, 0, Q, LO, moved),
                    (ka, 0, K, HI, moved), (ka, DH, K, LO, moved),
                ):
                    for odd in range(2):
                        src = slab[DH * odd:DH * odd + DH, which, part, :, :]
                        if tile is qm:
                            dst = qm[0:DH, odd:4:2, :]
                        else:
                            dst = tile[rows:rows + DH, p, 4 * g + odd:4 * g + 4:2, :]
                        sp.dma_start(dst, src).then_inc(done[g], 16)

            def move_maxima(f, p, g):
                sp.wait_ge(m_free, m_max(f, g) + 1)
                sp.dma_start(qb[DH + 1:DH + 2, p, 4 * g:4 * g + 4, :], m_row[:, :]).then_inc(max_moved, 16)

            def store(b, p):
                sp.wait_ge(o_free, O_USES * (b + 1))
                sp.dma_start(out[b].rearrange("(t p) f -> p t f", p=P), x1[:, p]).then_inc(stored, 16)

            def first():
                sp.dma_start(ident[:], identity).then_inc(raw_loaded[0], 16)
                sp.dma_start(mask_rows, nodemask.rearrange("b (t p) -> (b t) p", p=P)).then_inc(raw_loaded[0], 16)
                sp.dma_start(raw_qkv, w_qkv.rearrange("(k p) n -> p k n", p=P)).then_inc(raw_loaded[1], 16)
                sp.dma_start(raw_out, w_out.rearrange("(t p) n -> p t n", p=P)).then_inc(raw_loaded[2], 16)
                sp.dma_start(raw_k0, k0.rearrange("(t p) n -> p t n", p=P)).then_inc(raw_loaded[3], 16)
                load_x(0)
                load_adj(0)
                sp.dma_start(b_bc[:], b_out.unsqueeze(0).to_broadcast([P, D])).then_inc(raw_loaded[4], 16)
                sp.wait_ge(setup_dve, 2)
                sp.dma_start(bias_rows.rearrange("b (t p) -> (b t) p", p=P), mask_bias).then_inc(bias_stored, 16)
                sp.wait_ge(bias_stored, 16)
                load_adj(1)
                load_x(1)
                move_mask_bias(0, 0)
                move_heads(0, 0, 0)
                move_maxima(0, 0, 0)
                move_heads(0, 0, 1)

            def body(b, p):
                if after_first(b):
                    store(b - 1, 1 - p)
                move_maxima(b, p, 1)
                if has_load(b):
                    load_adj(b + 2)
                    load_x(b + 2)
                if has_front(b):
                    move_mask_bias(b + 1, 1 - p)
                    move_heads(b + 1, 1 - p, 0)
                    move_maxima(b + 1, 1 - p, 0)
                    move_heads(b + 1, 1 - p, 1)

            entries(sp, body, first)
            store(B - 1, (B - 1) % 2)
            sp.wait_ge(stored, 16 * B)

        @block.tensor
        def _(pe):
            def split_mm(dst, lhs, rhs, tiles, open_group=True, close_group=True):
                steps = [(i, a, c) for i in range(tiles) for a, c in PRODUCTS]
                for n, (i, a, c) in enumerate(steps):
                    last = nc.tensor.matmul(dst, lhs(a, i), rhs(c, i), start=open_group and n == 0,
                                            stop=close_group and n == len(steps) - 1)
                return last

            def f_bank(f, i):
                wait(pe, f_free[i % 2], F_USES // 2 * f + i // 2)
                return f_ps[:, i % 2, :]

            def both_evacuated(f, i):
                pe.wait_ge(f_free[0], f_count(f, i - 1))
                pe.wait_ge(f_free[1], f_count(f, i))

            def adj_transposes(f, tiles):
                if 0 in tiles:
                    pe.wait_ge(adj_loaded, 16 * (f + 1))
                for jt in tiles:
                    bank = f_bank(f, F_ADJ + jt)
                    for it in range(NT):
                        last = nc.tensor.transpose(bank[:, it * P:(it + 1) * P],
                                                   adj_sb[:, it, jt * P:(jt + 1) * P], ident[:])
                    last.then_inc(f_full, 1)

            def adj_h1(f, ft):
                if ft == 0:
                    both_evacuated(f, F_T - 1)
                    pe.wait_ge(h_lo, 2 * f + 1)
                bank = f_bank(f, F_T + ft)
                split_mm(bank, lambda a, i: h_s[:, a, i, ft * P:(ft + 1) * P],
                         lambda c, i: adjT[:, c, i, :], NT).then_inc(f_full, 1)

            def t_kernel(f):
                both_evacuated(f, F_Y - 1)
                for half in range(2):
                    bank = f_bank(f, F_Y + half)
                    for k in range(2):
                        it = 2 * half + k
                        last = split_mm(bank[:, k * D:(k + 1) * D],
                                        lambda a, i: hT[:, a, i, it * P:(it + 1) * P],
                                        lambda c, i: wk0[:, c, i, :], KT)
                    last.then_inc(f_full, 1)

            def h2_transposes(f):
                banks = [f_bank(f, F_H2 + ft) for ft in range(KT)]
                for it in range(NT):
                    pe.wait_ge(ln_relu, 2 * NT * f + NT + it + 1)
                    for ft in range(KT):
                        last = nc.tensor.transpose(banks[ft][:, it * P:(it + 1) * P],
                                                   h_f[:, it, ft * P:(ft + 1) * P], ident[:])
                        if it == NT - 1:
                            last.then_inc(f_full, 1)

            def queries_keys(f, pair):
                if pair == 0:
                    both_evacuated(f, F_H2 + 1)
                for which in (Q, K):
                    bank = f_bank(f, F_PAIR[pair] + which)
                    split_mm(bank, lambda a, i: wqkv[:, a, i, which, pair * P:(pair + 1) * P],
                             lambda c, i: hT[:, c, i, :], KT).then_inc(f_full, 1)

            def values(f, tiles):
                for jt in tiles:
                    bank = f_bank(f, F_V + jt)
                    split_mm(bank, lambda a, i: hT[:, a, i, jt * P:(jt + 1) * P],
                             lambda c, i: wqkv[:, c, i, V, :], KT).then_inc(f_full, 1)

            def u_product(f, ft):
                if ft == 0:
                    pe.wait_ge(g_lo, NT * (f + 1))
                    pe.wait_ge(h_lo, 2 * f + 2)
                bank = f_bank(f, F_U + ft)
                split_mm(bank, lambda a, i: h_s[:, a, i, ft * P:(ft + 1) * P],
                         lambda c, i: gT[:, c, i, :], NT).then_inc(f_full, 1)

            def blend_row(f):
                pe.wait_ge(mean_ready, f + 1)
                wait(pe, m_free, m_blend(f))
                split_mm(m_ps[:, 0:D], lambda a, i: mean_rep[:, a, i, :],
                         lambda c, i: wc[:, c, i, :], KT).then_inc(m_full, 1)

            def maxima_step(f, p, g, j):
                h = 4 * g + j // 2
                if j == 0:
                    if g == 0:
                        pe.wait_ge(bias_moved, 16 * (f + 1))
                    pe.wait_ge(keys_moved[g], 4 * 16 * (f + 1))
                wait(pe, s_free[j % 2], s_before(s_max(f, g, j), j % 2))
                for k in range(2):
                    it = 2 * (j % 2) + k
                    last = nc.tensor.matmul(s_ps[:, j % 2, k, :], qm[0:DH + 1, h % 4, it * P:(it + 1) * P],
                                            km[0:DH + 1, p, h, :], start=True, stop=True)
                last.then_inc(s_full, 1)

            def maxima_transpose(f, g):
                pe.wait_ge(s_free[1], s_before(s_max(f, g, 7), 1) + 1)
                wait(pe, m_free, m_max(f, g))
                for it in range(NT):
                    last = nc.tensor.transpose(m_ps[0:HEADS // 2, it * P:(it + 1) * P],
                                               maxima[:, 4 * g:4 * g + 4, it], ident[:])
                last.then_inc(m_full, 1)

            def scores(b, p, h, half):
                if h % 4 == 0 and half == 0:
                    g = h // 4
                    pe.wait_ge(moved[g], 10 * 16 * (b + 1))
                    pe.wait_ge(max_moved, 16 * (2 * b + g + 1))
                wait(pe, s_free[half], s_before(s_score(b, h, half), half))
                for k in range(2):
                    cols = slice((2 * half + k) * P, (2 * half + k + 1) * P)
                    nc.tensor.matmul(s_ps[:, half, k, :], ka[:, p, h, cols], qa[:, p, h, :],
                                     start=True, stop=False)
                    last = nc.tensor.matmul(s_ps[:, half, k, :], km[0:DH + 2, p, h, cols],
                                            qb[0:DH + 2, p, h, :], start=False, stop=True)
                last.then_inc(s_full, 1)

            def attend(b, p, h):
                if h == 0:
                    both_evacuated(b, F_V + NT - 1)
                wait(pe, o_free, O_USES * b + h)
                for half in range(2):
                    pe.wait_ge(p_lo[half], HEADS * b + h + 1)
                    for k in range(2):
                        jt = 2 * half + k
                        for it in range(NT):
                            dst = o_ps[:, it * (DH + 1):(it + 1) * (DH + 1)]
                            cols = slice(k * N + it * P, k * N + (it + 1) * P)
                            hi = p_s[:, h % 2, half, HI, cols]
                            lo = p_s[:, h % 2, half, LO, cols]
                            nc.tensor.matmul(dst, hi, vh[:, p, jt, h, 0:DH + 1],
                                             start=jt == 0 and it == 0, stop=False, skip_group_check=True)
                            nc.tensor.matmul(dst[:, 0:DH], hi, vl[:, p, jt, h, :],
                                             start=False, stop=False, skip_group_check=True)
                            last = nc.tensor.matmul(dst, lo, vh[:, p, jt, h, 0:DH + 1],
                                                    start=False, stop=jt == NT - 1, skip_group_check=True)
                last.then_inc(o_full, 1)

            def pair_transposes(b, t):
                pe.wait_ge(o_free, O_USES * b + 2 * t + 2)
                wait(pe, m_free, m_pair(b, t))
                for it in range(NT):
                    last = nc.tensor.transpose(m_ps[:, it * P:(it + 1) * P], o_pair[:, it, :], ident[:])
                last.then_inc(m_full, 1)

            def projection(b, half):
                pe.wait_ge(o_free, O_USES * b + HEADS + half)
                if half == 0:
                    both_evacuated(b, F_U + 1)
                    pe.wait_ge(m_free, m_pair(b, PAIRS - 1) + 1)
                for k in range(2):
                    it = 2 * half + k
                    rows = slice(it * P, (it + 1) * P)
                    dst = o_ps[:, k * D:(k + 1) * D]
                    split_mm(dst, lambda a, i: uT[:, a, i, rows], lambda c, i: wc[:, c, i, :], KT,
                             close_group=False)
                    last = split_mm(dst, lambda a, i: oT[:, a, i, rows], lambda c, i: wo[:, c, i, :],
                                    PAIRS, open_group=False)
                last.then_inc(o_full, 1)

            def first():
                pe.wait_ge(raw_loaded[0], 32)
                pe.wait_ge(setup_dve, 1)
                nc.tensor.transpose(m_ps[:, 0:B * NT], mask_f, ident[0:B * NT, 0:B * NT]).then_inc(setup_pe, 1)
                pe.wait_ge(setup_act, 1)
                for t in range(NT):
                    for kt in range(KT):
                        last = nc.tensor.transpose(
                            f_ps[:, t // 2, (t % 2) * D + kt * P:(t % 2) * D + (kt + 1) * P],
                            raw_v[:, kt, t * P:(t + 1) * P], ident[:])
                last.then_inc(setup_pe, 1)
                pe.wait_ge(setup_act, 2)
                pe.wait_ge(setup_dve, 3)
                for kt in range(KT):
                    for t in range(NT):
                        last = nc.tensor.matmul(o_ps[:, kt * D:(kt + 1) * D], wvT[:, t, kt * P:(kt + 1) * P],
                                                raw_out[:, t, :], start=t == 0, stop=t == NT - 1)
                last.then_inc(setup_pe, 1)
                pe.wait_ge(setup_dve, 5)
                adj_transposes(0, range(NT))
                adj_h1(0, 0)
                adj_h1(0, 1)
                t_kernel(0)
                h2_transposes(0)
                blend_row(0)
                queries_keys(0, 0)
                queries_keys(0, 1)
                values(0, range(NT))
                for j in range(4):
                    maxima_step(0, 0, 0, j)
                queries_keys(0, 2)
                for j in range(4, 8):
                    maxima_step(0, 0, 0, j)
                maxima_transpose(0, 0)
                queries_keys(0, 3)

            def body(b, p):
                f, q = b + 1, 1 - p
                front, before = has_front(b), after_first(b)
                if before:
                    attend(b - 1, q, HEADS - 1)
                scores(b, p, 0, 0)
                scores(b, p, 0, 1)
                if before:
                    pair_transposes(b - 1, PAIRS - 1)
                    projection(b - 1, 0)
                scores(b, p, 1, 0)
                scores(b, p, 1, 1)
                maxima_step(b, p, 1, 0)
                maxima_step(b, p, 1, 1)
                if before:
                    projection(b - 1, 1)
                maxima_step(b, p, 1, 2)
                maxima_step(b, p, 1, 3)
                u_product(b, 0)
                attend(b, p, 0)
                scores(b, p, 2, 0)
                scores(b, p, 2, 1)
                u_product(b, 1)
                maxima_step(b, p, 1, 4)
                maxima_step(b, p, 1, 5)
                if front:
                    adj_transposes(f, (0, 1))
                attend(b, p, 1)
                maxima_step(b, p, 1, 6)
                maxima_step(b, p, 1, 7)
                if front:
                    adj_transposes(f, (2,))
                scores(b, p, 3, 0)
                if front:
                    adj_transposes(f, (3,))
                scores(b, p, 3, 1)
                maxima_transpose(b, 1)
                attend(b, p, 2)
                if front:
                    adj_h1(f, 0)
                pair_transposes(b, 0)
                if front:
                    adj_h1(f, 1)
                scores(b, p, 4, 0)
                scores(b, p, 4, 1)
                if front:
                    t_kernel(f)
                attend(b, p, 3)
                scores(b, p, 5, 0)
                scores(b, p, 5, 1)
                pair_transposes(b, 1)
                attend(b, p, 4)
                if front:
                    h2_transposes(f)
                    blend_row(f)
                    queries_keys(f, 0)
                    queries_keys(f, 1)
                scores(b, p, 6, 0)
                scores(b, p, 6, 1)
                if front:
                    values(f, (0, 1))
                attend(b, p, 5)
                if front:
                    maxima_step(f, q, 0, 0)
                    maxima_step(f, q, 0, 1)
                    values(f, (2,))
                    maxima_step(f, q, 0, 2)
                    maxima_step(f, q, 0, 3)
                    values(f, (3,))
                scores(b, p, 7, 0)
                scores(b, p, 7, 1)
                pair_transposes(b, 2)
                if front:
                    maxima_step(f, q, 0, 4)
                    maxima_step(f, q, 0, 5)
                    queries_keys(f, 2)
                    maxima_step(f, q, 0, 6)
                    maxima_step(f, q, 0, 7)
                attend(b, p, 6)
                if front:
                    maxima_transpose(f, 0)
                    queries_keys(f, 3)

            entries(pe, body, first)
            attend(B - 1, (B - 1) % 2, HEADS - 1)
            pair_transposes(B - 1, PAIRS - 1)
            projection(B - 1, 0)
            projection(B - 1, 1)

        @block.scalar
        def _(act):
            def relu_norm(f, p, layer):
                act.wait_ge(ln_bias, 2 * f + layer + 1)
                src = xin if layer == 0 else x1[:, p]
                if layer == 0:
                    wait(act, f_full, F_USES * (f - 1) + F_H2 + 2)
                    wait(act, h_lo, 2 * f)
                for t in range(NT):
                    nc.scalar.activation(h_f[:, t, :], src[:, t, :], ACT.Relu, bias=nbias[:, t:t + 1],
                                         scale=rstd[:, t:t + 1],
                                         accum_out=h_sum[:, t:t + 1] if layer == 0 else None,
                                         ).then_inc(ln_relu, 1)

            def split_hi(f, i, dst, scale=1.0, **more):
                act.wait_ge(f_full, F_USES * f + i + 1)
                nc.scalar.activation(dst, f_ps[:, i % 2, :], ACT.Copy, scale=scale, **more).then_inc(f_hi, 1)

            def adj_parts(f, p, tiles):
                act.wait_ge(par_ready, f + 1)
                for jt in tiles:
                    i = F_ADJ + jt
                    act.wait_ge(f_full, F_USES * f + i + 1)
                    nc.scalar.activation(adjT[:, HI, jt, :], f_ps[:, i % 2, :], ACT.Copy)
                    wait(act, g_lo, NT * f + jt - 1)
                    nc.scalar.activation(e_sb[:, jt % 2, :], f_ps[:, i % 2, :], ACT.Exp, scale=-1.0,
                                         bias=par[:, p, 1, jt:jt + 1]).then_inc(f_hi, 1)

            def hi_t(f, ft):
                split_hi(f, F_T + ft, hT[:, HI, ft, :])

            def relu_y(f):
                act.wait_ge(row_used_ready, f + 1)
                for half in range(2):
                    i = F_Y + half
                    act.wait_ge(f_full, F_USES * f + i + 1)
                    for k in range(2):
                        it = 2 * half + k
                        last = nc.scalar.activation(h_f[:, it, :], f_ps[:, i % 2, k * D:(k + 1) * D], ACT.Relu,
                                                    scale=row_used[:, it:it + 1])
                    last.then_inc(f_free[i % 2], 1)

            def hi_h2T(f):
                for ft in range(KT):
                    split_hi(f, F_H2 + ft, hT[:, HI, ft, :], accum_out=f_sum[:, ft:ft + 1])

            def hi_pair(f, pair):
                if pair == 0:
                    wait(act, moved[1], 10 * 16 * f)
                    wait(act, keys_moved[1], 4 * 16 * f)
                if pair == 2:
                    act.wait_ge(moved[0], 10 * 16 * (f + 1))
                    act.wait_ge(keys_moved[0], 4 * 16 * (f + 1))
                for which in (Q, K):
                    split_hi(f, F_PAIR[pair] + which, slab[:, which, HI, pair % 2, :], scale=1 / W_SCALE)

            def hi_values(f, p, tiles):
                for jt in tiles:
                    i = F_V + jt
                    act.wait_ge(f_full, F_USES * f + i + 1)
                    nc.scalar.activation(vh[:, p, jt, :, 0:DH],
                                         f_ps[:, i % 2, :].rearrange("p (h d) -> p h d", d=DH),
                                         ACT.Copy, scale=1 / W_SCALE).then_inc(f_hi, 1)

            def hi_u(f, ft):
                split_hi(f, F_U + ft, uT[:, HI, ft, :])

            def negate_maxima(f, g):
                act.wait_ge(m_full, m_max(f, g) + 1)
                wait(act, max_moved, 16 * (2 * f + g))
                nc.scalar.activation(m_row[:, :], m_ps[0:HEADS // 2, :], ACT.Copy,
                                     scale=-1.0).then_inc(m_free, 1)

            def exponentials(b, h, halves=(0, 1)):
                for half in halves:
                    act.wait_ge(s_full, s_score(b, h, half) + 1)
                    wait(act, p_lo[half], HEADS * b + h)
                    nc.scalar.activation(p_f[:, half, :].rearrange("p (k n) -> p k n", k=2), s_ps[:, half],
                                         ACT.Exp, scale=DH ** -0.5).then_inc(s_free[half], 1)

            def hi_pair_out(b, t):
                act.wait_ge(m_full, m_pair(b, t) + 1)
                nc.scalar.activation(oT[:, HI, t, :], m_ps[:], ACT.Copy).then_inc(m_hi, 1)

            def first():
                act.wait_ge(raw_loaded[1], 16)
                for kt in range(KT):
                    src = raw_qkv[:, kt, :].rearrange("p (h three d) -> p h three d", three=3, d=DH)
                    nc.scalar.activation(raw_v[:, kt, :].rearrange("p (h d) -> p h d", d=DH), src[:, :, V, :],
                                         ACT.Copy)
                    for which in (Q, K, V):
                        src = raw_qkv[:, kt, :].rearrange("p (h three d) -> p h three d", three=3, d=DH)
                        last = nc.scalar.activation(
                            wqkv[:, HI, kt, which, :].rearrange("p (h d) -> p h d", d=DH),
                            src[:, :, which, :], ACT.Copy, scale=W_SCALE)
                last.then_inc(setup_act, 1)
                act.wait_ge(setup_pe, 2)
                for k in range(2):
                    last = nc.scalar.activation(
                        wvT[:, 2 * k:2 * k + 2, :],
                        f_ps[:, k, :].rearrange("p (t n) -> p t n", t=2), ACT.Copy)
                last.then_inc(setup_act, 1)
                act.wait_ge(setup_pe, 3)
                nc.scalar.activation(wc[:, HI], o_ps[:].rearrange("p (k n) -> p k n", k=KT),
                                     ACT.Copy).then_inc(setup_act, 1)
                relu_norm(0, 0, 0)
                act.wait_ge(bias_stored, 16)
                adj_parts(0, 0, range(NT))
                hi_t(0, 0)
                hi_t(0, 1)
                relu_y(0)
                relu_norm(0, 0, 1)
                hi_h2T(0)
                hi_pair(0, 0)
                hi_pair(0, 1)
                hi_values(0, 0, range(NT))
                hi_pair(0, 2)
                negate_maxima(0, 0)
                hi_pair(0, 3)

            def body(b, p):
                f, q = b + 1, 1 - p
                front, before = has_front(b), after_first(b)
                exponentials(b, 0)
                if front:
                    relu_norm(f, q, 0)
                if before:
                    hi_pair_out(b - 1, PAIRS - 1)
                exponentials(b, 1)
                hi_u(b, 0)
                exponentials(b, 2)
                hi_u(b, 1)
                if front:
                    adj_parts(f, q, (0, 1, 2))
                exponentials(b, 3, (0,))
                if front:
                    adj_parts(f, q, (3,))
                exponentials(b, 3, (1,))
                negate_maxima(b, 1)
                if front:
                    hi_t(f, 0)
                hi_pair_out(b, 0)
                if front:
                    hi_t(f, 1)
                exponentials(b, 4)
                if front:
                    relu_y(f)
                exponentials(b, 5)
                hi_pair_out(b, 1)
                if front:
                    relu_norm(f, q, 1)
                    hi_h2T(f)
                    hi_pair(f, 0)
                    hi_pair(f, 1)
                exponentials(b, 6)
                if front:
                    hi_values(f, q, range(NT))
                exponentials(b, 7)
                hi_pair_out(b, 2)
                if front:
                    hi_pair(f, 2)
                    negate_maxima(f, 0)
                    hi_pair(f, 3)

            entries(act, body, first)
            hi_pair_out(B - 1, PAIRS - 1)

        @block.vector
        def _(dve):
            def norm_stats(f, p, layer):
                k = 2 * f + layer + 1
                if layer == 0:
                    dve.wait_ge(x_loaded, 16 * (f + 1))
                else:
                    dve.wait_ge(y_added, 2 * (f + 1))
                src = xin if layer == 0 else x1[:, p]
                for t in range(NT):
                    last = nc.vector.bn_stats(stats[:, t, :], src[:, t, :])
                last.then_inc(ln_stats, 1)
                dve.wait_ge(ln_stats, k)
                nc.vector.memset(var_eps[:], EPS)
                for t in range(NT):
                    last = nc.vector.bn_aggr(meanvar[:, t, :], stats[:, t, :])
                last.then_inc(ln_aggr, 1)
                dve.wait_ge(ln_aggr, k)
                nc.vector.tensor_tensor(var_eps[:], meanvar[:, :, 1], var_eps[:], ALU.add).then_inc(ln_var, 1)

            def norm_bias(f, layer):
                dve.wait_ge(ln_rstd, 2 * f + layer + 1)
                nc.vector.scalar_tensor_tensor(nbias[:], meanvar[:, :, 0], -1.0, rstd[:], ALU.mult,
                                               ALU.mult).then_inc(ln_bias, 1)

            def h_high(f, layer):
                dve.wait_ge(ln_relu, NT * (2 * f + layer + 1))
                if layer == 0:
                    wait(dve, f_full, F_USES * f)
                    nc.vector.tensor_scalar(row_used[:], h_sum[:], 0.0, 1 / K_SCALE, ALU.is_gt,
                                            ALU.mult).then_inc(row_used_ready, 1)
                nc.vector.tensor_copy(h_s[:, HI], h_f[:]).then_inc(h_hi, 1)

            def split_lo(f, i, dst, hi, scale=None):
                dve.wait_ge(f_hi, hi_count(f, i))
                src = f_ps[:, i % 2, :]
                if scale is None:
                    return nc.vector.tensor_tensor(dst, src, hi, ALU.subtract)
                return nc.vector.scalar_tensor_tensor(dst, src, scale, hi, ALU.mult, ALU.subtract)

            def take_par(f, p):
                wait(dve, o_free, O_USES * (f - 1))
                nc.vector.tensor_copy(par[:, p].rearrange("p a t -> p (a t)"),
                                      par_all[:, f].rearrange("p a t -> p (a t)")).then_inc(par_ready, 1)

            def adj_parts(f, p, tiles):
                dve.wait_ge(par_ready, f + 1)
                for jt in tiles:
                    i = F_ADJ + jt
                    split_lo(f, i, adjT[:, LO, jt, :], adjT[:, HI, jt, :])
                    e = e_sb[:, jt % 2, :]
                    nc.vector.scalar_tensor_tensor(e, f_ps[:, i % 2, :], par[:, p, 0, jt:jt + 1], e,
                                                   ALU.mult, ALU.add).then_inc(f_free[i % 2], 1)
                    dve.wait_ge(f_free[i % 2], f_count(f, i))
                    nc.vector.tensor_copy(gT[:, HI, jt, :], e).then_inc(g_hi, 1)

            def lo_t(f, ft):
                i = F_T + ft
                split_lo(f, i, hT[:, LO, ft, :], hT[:, HI, ft, :]).then_inc(f_free[i % 2], 1)

            def add_y(f, p):
                wait(dve, stored, 16 * (f - 1))
                for half in range(2):
                    dve.wait_ge(f_free[half], f_count(f, F_Y + half))
                    rows = slice(2 * half, 2 * half + 2)
                    nc.vector.tensor_tensor(x1[:, p, rows, :], xin[:, rows, :], h_f[:, rows, :],
                                            ALU.add).then_inc(y_added, 1)

            def lo_h2T(f):
                for ft in range(KT):
                    i = F_H2 + ft
                    split_lo(f, i, hT[:, LO, ft, :], hT[:, HI, ft, :]).then_inc(f_free[i % 2], 1)
                for ft in range(KT):
                    last = nc.vector.tensor_scalar(mean_rep[:, HI, ft, :], ones[:], f_sum[:, ft:ft + 1], None,
                                                   ALU.mult)
                last.then_inc(mean_hi, 1)
                dve.wait_ge(mean_hi, f + 1)
                for ft in range(KT):
                    last = nc.vector.scalar_tensor_tensor(mean_rep[:, LO, ft, :], ones[:], f_sum[:, ft:ft + 1],
                                                          mean_rep[:, HI, ft, :], ALU.mult, ALU.subtract)
                last.then_inc(mean_ready, 1)

            def add_blend(f, p):
                dve.wait_ge(m_full, m_blend(f) + 1)
                dve.wait_ge(b_added, f + 1)
                for it in range(NT):
                    last = nc.vector.scalar_tensor_tensor(x1[:, p, it, :], m_ps[:, 0:D], par[:, p, 3, it:it + 1],
                                                          x1[:, p, it, :], ALU.mult, ALU.add)
                last.then_inc(m_free, 1)

            def lo_pair(f, pair):
                for which in (Q, K):
                    i = F_PAIR[pair] + which
                    split_lo(f, i, slab[:, which, LO, pair % 2, :], slab[:, which, HI, pair % 2, :],
                             1 / W_SCALE).then_inc(f_free[i % 2], 1)

            def lo_values(f, p, tiles):
                for jt in tiles:
                    i = F_V + jt
                    dve.wait_ge(f_hi, hi_count(f, i))
                    nc.vector.scalar_tensor_tensor(
                        vl[:, p, jt], f_ps[:, i % 2, :].rearrange("p (h d) -> p h d", d=DH), 1 / W_SCALE,
                        vh[:, p, jt, :, 0:DH], ALU.mult, ALU.subtract).then_inc(f_free[i % 2], 1)

            def lo_u(f, ft):
                i = F_U + ft
                split_lo(f, i, uT[:, LO, ft, :], uT[:, HI, ft, :]).then_inc(f_free[i % 2], 1)

            def take_maxima(f, g, steps):
                for j in steps:
                    dve.wait_ge(s_full, s_max(f, g, j) + 1)
                    its = slice(2 * (j % 2), 2 * (j % 2) + 2)
                    nc.vector.reduce_max(maxima[:, 4 * g + j // 2, its], s_ps[:, j % 2],
                                         AX_X).then_inc(s_free[j % 2], 1)

            def split_p(b, h):
                wait(dve, o_full, O_USES * b + h - 1 if h >= 2 else O_USES * (b - 1) + HEADS - 1 + h)
                for half in range(2):
                    dve.wait_ge(s_free[half], s_before(s_score(b, h, half), half) + 1)
                    nc.vector.tensor_copy(p_s[:, h % 2, half, HI, :], p_f[:, half, :]).then_inc(p_hi, 1)
                if h not in POOL_HEADS:
                    dve.wait_ge(p_hi, 2 * (HEADS * b + h) + 2)
                    nc.vector.tensor_tensor(p_s[:, h % 2, 1, LO, :], p_f[:, 1, :], p_s[:, h % 2, 1, HI, :],
                                            ALU.subtract).then_inc(p_lo[1], 1)

            def divide(b, h):
                dve.wait_ge(o_full, O_USES * b + h + 1)
                o = o_ps[:, 0:NT * (DH + 1)].rearrange("p (t d) -> p t d", t=NT)
                nc.vector.reciprocal(recip[:].unsqueeze(2), o[:, :, DH:DH + 1]).then_inc(recip_done, 1)
                dve.wait_ge(recip_done, HEADS * b + h + 1)
                if h % 2 == 0:
                    if h:
                        dve.wait_ge(m_full, m_pair(b, h // 2 - 1) + 1)
                    else:
                        wait(dve, m_full, m_pair(b - 1, PAIRS - 1) + 1 if after_first(b) else 0)
                nc.vector.tensor_tensor(o_pair[:, :, (h % 2) * DH:(h % 2 + 1) * DH], o[:, :, 0:DH],
                                        recip[:].unsqueeze(2).to_broadcast([P, NT, DH]),
                                        ALU.mult).then_inc(o_free, 1)

            def lo_pair_out(b, t):
                dve.wait_ge(m_hi, PAIRS * b + t + 1)
                nc.vector.tensor_tensor(oT[:, LO, t, :], m_ps[:], oT[:, HI, t, :],
                                        ALU.subtract).then_inc(m_free, 1)

            def add_projection(b, p, half):
                dve.wait_ge(o_full, O_USES * b + HEADS + half + 1)
                for k in range(2):
                    it = 2 * half + k
                    last = nc.vector.scalar_tensor_tensor(x1[:, p, it, :], o_ps[:, k * D:(k + 1) * D],
                                                          par[:, p, 2, it:it + 1], x1[:, p, it, :],
                                                          ALU.mult, ALU.add)
                last.then_inc(o_free, 1)

            def first():
                nc.vector.memset(minus_half[:], -0.5)
                nc.vector.memset(km[DH:DH + 2], 1.0)
                nc.vector.memset(qb[DH:DH + 2], 1.0)
                nc.vector.memset(qm[DH:DH + 1], 1.0)
                nc.vector.memset(vh[:, :, :, :, DH:DH + 2], 1.0)
                nc.vector.memset(ones[:], 1.0)
                dve.wait_ge(raw_loaded[0], 32)
                nc.vector.tensor_copy(mask_f, mask_rows).then_inc(setup_dve, 1)
                dve.wait_ge(setup_dve, 1)
                nc.vector.tensor_scalar(mask_bias, mask_f, MASKED, -MASKED, ALU.mult,
                                        ALU.add).then_inc(setup_dve, 1)
                dve.wait_ge(raw_loaded[2], 16)
                nc.vector.tensor_scalar(raw_out, raw_out, LAMBDA * W_SCALE, None, ALU.mult).then_inc(setup_dve, 1)
                dve.wait_ge(setup_pe, 1)
                m = m_ps[:, 0:B * NT].rearrange("p (b t) -> p b t", t=NT)
                for kind, (a, c) in enumerate(((1.0, 0.0), (GONE, -GONE), (1 / W_SCALE, 0.0),
                                               (-1 / (W_SCALE * N), 1 / (W_SCALE * N)))):
                    nc.vector.tensor_scalar(par_all[:, :, kind, :], m, a, c, ALU.mult, ALU.add)
                dve.wait_ge(setup_act, 1)
                for kt in range(KT):
                    for which in (Q, K, V):
                        src = raw_qkv[:, kt, :].rearrange("p (h three d) -> p h three d", three=3, d=DH)
                        nc.vector.scalar_tensor_tensor(
                            wqkv[:, LO, kt, which, :].rearrange("p (h d) -> p h d", d=DH), src[:, :, which, :],
                            W_SCALE, wqkv[:, HI, kt, which, :].rearrange("p (h d) -> p h d", d=DH),
                            ALU.mult, ALU.subtract)
                dve.wait_ge(raw_loaded[3], 16)
                dve.wait_ge(setup_dve, 3)
                nc.vector.tensor_scalar(wk0[:, HI], raw_k0, K_SCALE, None, ALU.mult)
                nc.vector.tensor_copy(wo[:, HI], raw_out).then_inc(setup_dve, 1)
                dve.wait_ge(setup_dve, 4)
                nc.vector.scalar_tensor_tensor(wk0[:, LO], raw_k0, K_SCALE, wk0[:, HI], ALU.mult, ALU.subtract)
                nc.vector.tensor_tensor(wo[:, LO], raw_out, wo[:, HI], ALU.subtract)
                dve.wait_ge(setup_act, 3)
                nc.vector.tensor_tensor(wc[:, LO], o_ps[:].rearrange("p (k n) -> p k n", k=KT), wc[:, HI],
                                        ALU.subtract).then_inc(setup_dve, 1)
                dve.wait_ge(setup_dve, 5)
                take_par(0, 0)
                norm_stats(0, 0, 0)
                norm_bias(0, 0)
                h_high(0, 0)
                adj_parts(0, 0, range(NT))
                lo_t(0, 0)
                lo_t(0, 1)
                add_y(0, 0)
                norm_stats(0, 0, 1)
                norm_bias(0, 1)
                h_high(0, 1)
                lo_h2T(0)
                add_blend(0, 0)
                lo_pair(0, 0)
                lo_pair(0, 1)
                lo_values(0, 0, range(NT))
                take_maxima(0, 0, range(4))
                lo_pair(0, 2)
                take_maxima(0, 0, range(4, 8))
                lo_pair(0, 3)

            def body(b, p):
                f, q = b + 1, 1 - p
                front, before = has_front(b), after_first(b)
                if front:
                    norm_stats(f, q, 0)
                if before:
                    divide(b - 1, HEADS - 1)
                split_p(b, 0)
                if front:
                    norm_bias(f, 0)
                if before:
                    lo_pair_out(b - 1, PAIRS - 1)
                    add_projection(b - 1, q, 0)
                split_p(b, 1)
                take_maxima(b, 1, (0, 1))
                if before:
                    add_projection(b - 1, q, 1)
                take_maxima(b, 1, (2, 3))
                if front:
                    take_par(f, q)
                lo_u(b, 0)
                divide(b, 0)
                split_p(b, 2)
                lo_u(b, 1)
                if front:
                    h_high(f, 0)
                take_maxima(b, 1, (4, 5))
                if front:
                    adj_parts(f, q, (0, 1))
                divide(b, 1)
                take_maxima(b, 1, (6, 7))
                if front:
                    adj_parts(f, q, (2, 3))
                split_p(b, 3)
                divide(b, 2)
                if front:
                    lo_t(f, 0)
                lo_pair_out(b, 0)
                if front:
                    lo_t(f, 1)
                split_p(b, 4)
                if front:
                    add_y(f, q)
                    norm_stats(f, q, 1)
                divide(b, 3)
                if front:
                    norm_bias(f, 1)
                split_p(b, 5)
                lo_pair_out(b, 1)
                divide(b, 4)
                if front:
                    h_high(f, 1)
                    lo_h2T(f)
                    add_blend(f, q)
                    lo_pair(f, 0)
                    lo_pair(f, 1)
                split_p(b, 6)
                if front:
                    lo_values(f, q, (0, 1))
                divide(b, 5)
                if front:
                    take_maxima(f, 0, (0, 1))
                    lo_values(f, q, (2,))
                    take_maxima(f, 0, (2, 3))
                    lo_values(f, q, (3,))
                split_p(b, 7)
                lo_pair_out(b, 2)
                if front:
                    take_maxima(f, 0, (4, 5))
                    lo_pair(f, 2)
                    take_maxima(f, 0, (6, 7))
                divide(b, 6)
                if front:
                    lo_pair(f, 3)

            entries(dve, body, first)
            divide(B - 1, HEADS - 1)
            lo_pair_out(B - 1, PAIRS - 1)
            add_projection(B - 1, (B - 1) % 2, 0)
            add_projection(B - 1, (B - 1) % 2, 1)

        @block.gpsimd
        def _(pool):
            def norm_rstd(f, layer):
                pool.wait_ge(ln_var, 2 * f + layer + 1)
                nc.gpsimd.tensor_tensor(rstd[:], var_eps[:], minus_half[:], ALU.pow).then_inc(ln_rstd, 1)

            def h_low(f, layer):
                pool.wait_ge(h_hi, 2 * f + layer + 1)
                nc.gpsimd.tensor_tensor(h_s[:, LO], h_f[:], h_s[:, HI], ALU.subtract).then_inc(h_lo, 1)

            def g_low(f):
                for jt in range(NT):
                    pool.wait_ge(g_hi, NT * f + jt + 1)
                    nc.gpsimd.tensor_tensor(gT[:, LO, jt, :], e_sb[:, jt % 2, :], gT[:, HI, jt, :],
                                            ALU.subtract).then_inc(g_lo, 1)

            def add_b(f, p):
                pool.wait_ge(ln_relu, 2 * NT * (f + 1))
                pool.wait_ge(raw_loaded[4], 16)
                nc.gpsimd.tensor_tensor(x1[:, p], x1[:, p], b_bc[:].unsqueeze(1).to_broadcast([P, NT, D]),
                                        ALU.add).then_inc(b_added, 1)

            def p_low(b, h):
                for half in (0, 1) if h in POOL_HEADS else (0,):
                    pool.wait_ge(p_hi, 2 * (HEADS * b + h) + half + 1)
                    nc.gpsimd.tensor_tensor(p_s[:, h % 2, half, LO, :], p_f[:, half, :],
                                            p_s[:, h % 2, half, HI, :], ALU.subtract).then_inc(p_lo[half], 1)

            def first():
                norm_rstd(0, 0)
                h_low(0, 0)
                g_low(0)
                norm_rstd(0, 1)
                h_low(0, 1)
                add_b(0, 0)

            def body(b, p):
                f, q = b + 1, 1 - p
                front = has_front(b)
                if front:
                    norm_rstd(f, 0)
                p_low(b, 0)
                p_low(b, 1)
                if front:
                    h_low(f, 0)
                p_low(b, 2)
                if front:
                    g_low(f)
                p_low(b, 3)
                if front:
                    norm_rstd(f, 1)
                p_low(b, 4)
                if front:
                    h_low(f, 1)
                    add_b(f, q)
                p_low(b, 5)
                p_low(b, 6)
                p_low(b, 7)

            entries(pool, body, first)


_INS = ["x", "adj", "nodemask", "L0_gnn_kernel", "L1_gnn_W_qkv", "L1_gnn_W_out", "L1_gnn_b_out"]


def kernel(**inputs):
    import numpy as _np
    import concourse.bacc as _bacc
    from concourse import mybir as _mybir
    from concourse.bass_utils import run_bass_kernel_spmd as _run

    nc = _bacc.Bacc("TRN2", target_bir_lowering=False, num_devices=1)
    arrays, args = {}, []
    for name in _INS:
        a = _np.ascontiguousarray(inputs[name])
        if a.dtype == _np.bool_:
            a = a.view(_np.uint8)
        arrays[f"in_{name}"] = a
        args.append(nc.dram_tensor(f"in_{name}", a.shape, _mybir.dt.from_np(a.dtype), kind="ExternalInput").ap())
    eye = _np.eye(128, dtype=_np.float32)
    arrays["in_identity"] = eye
    args.append(nc.dram_tensor("in_identity", eye.shape, _mybir.dt.float32, kind="ExternalInput").ap())
    args.append(nc.dram_tensor("mask_bias_rows", inputs["nodemask"].shape, _mybir.dt.float16).ap())
    args.append(nc.dram_tensor("out_0", inputs["x"].shape, _mybir.dt.float32, kind="ExternalOutput").ap())
    gnn_kernel(nc, *args)
    r = _run(nc, [arrays], core_ids=[0])
    return r.results[0]["out_0"]
```

```python
from contextlib import ExitStack

import concourse.bass as bass
from concourse import mybir

F32 = mybir.dt.float32
F16 = mybir.dt.float16
U8 = mybir.dt.uint8
ALU = mybir.AluOpType
ACT = mybir.ActivationFunctionType
AX_X = mybir.AxisListType.X

P = 128
HEADS = 8
DH = 64
LAMBDA = 0.33
EPS = 1e-5

W_SCALE = 32.0
K_SCALE = 16.0
MASKED = 60000.0
GONE = 1e30

HI, LO = 0, 1
PRODUCTS = ((HI, HI), (HI, LO), (LO, HI))
Q, K, V = 0, 1, 2

F_ADJ, F_T, F_Y, F_H2, F_V, F_U, F_USES = 0, 4, 6, 8, 14, 22, 24
F_PAIR = (10, 12, 18, 20)
S_ORDER = (
    "h0 s0 h1 s1 s2 s3 h2 h3 h4 h5 h6 h7 f0 f1 f2 f3".split(),
    "h0 s0 s1 s2 h1 s3 h2 h3 h4 h5 h6 h7 f0 f1 f2 f3".split(),
)
S_USES, S_FIRST = 16, 4
M_ORDER = "p3 s p0 p1 u p2 f".split()
M_USES, M_FIRST = 7, 2
O_USES = HEADS + 2


def gnn_kernel(nc, x, adj, nodemask, k0, w_qkv, w_out, b_out, identity, bias_rows, out):
    B, N, D = x.shape
    NT = N // P
    KT = D // P
    PAIRS = HEADS // 2
    HALF = N * NT // 2
    assert (N, D, HEADS * DH) == (512, 256, 512)

    with ExitStack() as ctx:
        def sb(name, shape, dt):
            return ctx.enter_context(nc.sbuf_tensor(name, shape, dt))

        def psum(name, shape):
            return ctx.enter_context(nc.psum_tensor(name, shape, F32))

        def sem(name):
            return ctx.enter_context(nc.semaphore(name))

        ident = sb("ident", [P, P], F32)
        ones = sb("ones", [P, P], F16)
        wqkv = sb("wqkv", [P, 2, KT, 3, N], F16)
        wo = sb("wo", [P, 2, NT, D], F16)
        wk0 = sb("wk0", [P, 2, KT, D], F16)
        wc = sb("wc", [P, 2, KT, D], F16)
        b_bc = sb("b_bc", [P, D], F32)
        par_all = sb("par_all", [P, B, 4, NT], F32)
        par = sb("par", [P, 2, 4, NT], F32)

        xin = sb("xin", [P, NT, D], F32)
        x1 = sb("x1", [P, 2, NT, D], F32)
        adj_sb = sb("adj_sb", [P, NT, N], F32)
        adjT = sb("adjT", [P, 2, NT, N], F16)
        e_sb = sb("e_sb", [P, 2, N], F32)
        gT = sb("gT", [P, 2, NT, N], F16)
        h_f = sb("h_f", [P, NT, D], F32)
        h_s = sb("h_s", [P, 2, NT, D], F16)
        hT = sb("hT", [P, 2, KT, N], F16)
        uT = sb("uT", [P, 2, KT, N], F16)
        slab = sb("slab", [P, 2, 2, 2, N], F16)
        qm = sb("qm", [P, 4, N], F16)
        stats = sb("stats", [P, NT, 6], F32)
        meanvar = sb("meanvar", [P, NT, 2], F32)
        var_eps = sb("var_eps", [P, NT], F32)
        minus_half = sb("minus_half", [P, NT], F32)
        rstd = sb("rstd", [P, NT], F32)
        nbias = sb("nbias", [P, NT], F32)
        h_sum = sb("h_sum", [P, NT], F32)
        row_used = sb("row_used", [P, NT], F32)
        f_sum = sb("f_sum", [P, KT], F32)
        mean_rep = sb("mean_rep", [P, 2, KT, P], F16)
        maxima = sb("maxima", [P, HEADS, NT], F32)
        m_row = sb("m_row", [HEADS // 2 * NT, P], F16)

        ka = sb("ka", [P, 2, HEADS, N], F16)
        qa = sb("qa", [P, 2, HEADS, N], F16)
        km = sb("km", [P, 2, HEADS, N], F16)
        qb = sb("qb", [P, 2, HEADS, N], F16)
        vh = sb("vh", [P, 2, NT, HEADS, DH + 2], F16)
        vl = sb("vl", [P, 2, NT, HEADS, DH], F16)
        p_f = sb("p_f", [P, 2, HALF], F32)
        p_s = sb("p_s", [P, 2, 2, 2, HALF], F16)
        recip = sb("recip", [P, NT], F32)
        o_pair = sb("o_pair", [P, NT, P], F32)
        oT = sb("oT", [P, 2, PAIRS, N], F16)

        raw_qkv = p_s[:].rearrange("p a b c n -> p (a b c n)").bitcast(F32)[:, 0:KT * 3 * N].rearrange(
            "p (k n) -> p k n", k=KT)
        raw_out = p_f[:, 0, :].rearrange("p (t n) -> p t n", t=NT)
        raw_k0 = p_f[:, 1, 0:KT * D].rearrange("p (t n) -> p t n", t=KT)
        raw_v = x1[:, 1].rearrange("p t n -> p (t n)").rearrange("p (k n) -> p k n", k=KT)
        wvT = uT[:].rearrange("p a t n -> p (a t n)").bitcast(F32)[:, 0:NT * D].rearrange(
            "p (t n) -> p t n", t=NT)

        mask_f = o_pair[0:B * NT, 0, :]
        mask_bias = o_pair[0:B * NT, 1, 0:P // 2].bitcast(F16)
        mask_rows = o_pair[0:B * NT, 2, 0:P // 4].bitcast(U8)

        s_ps = psum("s_ps", [P, 2, 2, N])
        f_ps = psum("f_ps", [P, 2, N])
        m_ps = psum("m_ps", [P, N])
        o_ps = psum("o_ps", [P, N])

        raw_loaded = [sem(f"raw_loaded{i}") for i in range(5)]
        ones_ready = sem("ones_ready")
        ones_placed = sem("ones_placed")
        mask_cast = sem("mask_cast")
        mask_biased = sem("mask_biased")
        mask_turned = sem("mask_turned")
        columns_ready = sem("columns_ready")
        kernel_high = sem("kernel_high")
        kernel_split = sem("kernel_split")
        wo_scaled = sem("wo_scaled")
        wo_high = sem("wo_high")
        wv_gathered = sem("wv_gathered")
        qkv_high = sem("qkv_high")
        qkv_split = sem("qkv_split")
        wvT_full = sem("wvT_full")
        wvT_copied = sem("wvT_copied")
        wc_full = sem("wc_full")
        wc_high = sem("wc_high")
        wc_split = sem("wc_split")
        bias_stored = sem("bias_stored")
        x_loaded = sem("x_loaded")
        adj_loaded = sem("adj_loaded")
        par_ready = sem("par_ready")
        ln_stats = sem("ln_stats")
        ln_aggr = sem("ln_aggr")
        ln_var = sem("ln_var")
        ln_rstd = sem("ln_rstd")
        ln_bias = sem("ln_bias")
        ln_relu = sem("ln_relu")
        row_used_ready = sem("row_used_ready")
        h_hi = sem("h_hi")
        h_lo = sem("h_lo")
        f_full = sem("f_full")
        f_hi = sem("f_hi")
        f_free = [sem("f_free0"), sem("f_free1")]
        g_hi = sem("g_hi")
        g_lo = sem("g_lo")
        y_added = sem("y_added")
        b_added = sem("b_added")
        mean_hi = sem("mean_hi")
        mean_ready = sem("mean_ready")
        moved = [sem("moved0"), sem("moved1")]
        keys_moved = [sem("keys_moved0"), sem("keys_moved1")]
        bias_moved = sem("bias_moved")
        max_moved = sem("max_moved")
        m_full = sem("m_full")
        m_hi = sem("m_hi")
        m_free = sem("m_free")
        s_full = [sem("s_full0"), sem("s_full1")]
        s_free = [sem("s_free0"), sem("s_free1")]
        p_hi = [sem("p_hi0"), sem("p_hi1")]
        p_lo = [sem("p_lo0"), sem("p_lo1")]
        o_full = sem("o_full")
        o_free = sem("o_free")
        recip_done = sem("recip_done")
        stored = sem("stored")

        def wait(eng, s, value):
            if not (isinstance(value, int) and value <= 0):
                eng.wait_ge(s, value)

        def is_last(b):
            return isinstance(b, int) and b == B - 1

        def m_use(b, label):
            at = M_ORDER.index(label)
            if not after_first(b):
                return M_FIRST + at - (at > M_ORDER.index("p3"))
            if is_last(b):
                at -= sum(M_ORDER.index(k) < at for k in ("u", "f"))
            return M_FIRST - 1 + M_USES * b + at

        def m_pair(b, t):
            if t < PAIRS - 1:
                return m_use(b, f"p{t}")
            return M_FIRST - 1 + M_USES * (b + 1) - 2 if is_last(b) else m_use(b + 1, "p3")

        def m_blend(f):
            return 0 if isinstance(f, int) and f == 0 else m_use(f - 1, "u")

        def m_max(f, g):
            if g == 1:
                return m_use(f, "s")
            return 1 if isinstance(f, int) and f == 0 else m_use(f - 1, "f")

        def s_use(b, half, label):
            at = S_ORDER[half].index(label)
            if is_last(b):
                at -= sum(k[0] == "f" for k in S_ORDER[half][:at])
            return S_FIRST + S_USES * b + at

        def s_score(b, h, half):
            return s_use(b, half, f"h{h}")

        def s_max(f, g, j):
            if g == 1:
                return s_use(f, j % 2, f"s{j // 2}")
            return j // 2 if isinstance(f, int) and f == 0 else s_use(f - 1, j % 2, f"f{j // 2}")

        def before_head(b, h):
            return O_USES * b + h - 1 if h >= 2 else O_USES * (b - 1) + HEADS - 1 + h

        def f_count(f, i):
            return F_USES // 2 * f + i // 2 + 1

        def hi_count(f, i):
            return (F_USES - 2) * f + (i if i < F_Y else i - 2) + 1

        LOOP = (1, B - 3)

        def entries(eng, body, first):
            first()
            body(0, 0)
            with eng.Fori(0, (LOOP[1] - LOOP[0]) // 2) as turn:
                for k in range(2):
                    body(turn * 2 + (1 + k), (1 + k) % 2)
            for b in range(LOOP[1], B):
                body(b, b % 2)

        def has_front(b):
            return not (isinstance(b, int) and b + 1 >= B)

        def has_load(b):
            return not (isinstance(b, int) and b + 2 >= B)

        def after_first(b):
            return not (isinstance(b, int) and b == 0)

        ctx.enter_context(nc.allow_non_contiguous_dma(reason="mask rows and head placement"))
        block = ctx.enter_context(nc.Block())

        @block.sync
        def _(sp):
            def load_x(f):
                wait(sp, y_added, 2 * f)
                sp.dma_start(xin[:], x[f].rearrange("(t p) f -> p t f", p=P)).then_inc(x_loaded, 16)

            def load_adj(f):
                wait(sp, f_full, F_USES * (f - 1) + F_T)
                sp.dma_start(adj_sb[:], adj[f].rearrange("(t p) m -> p t m", p=P)).then_inc(adj_loaded, 16)

            def move_mask_bias(f, p):
                wait(sp, f_full, F_USES * f + F_PAIR[0] + 1)
                row = bias_rows[f].unsqueeze(0).unsqueeze(0)
                sp.dma_start(km[DH:DH + 1, p, :, :], row.to_broadcast([1, HEADS, N])).then_inc(bias_moved, 16)

            def move_heads(f, p, g):
                sp.wait_ge(f_free[0], f_count(f, F_PAIR[2 * g + 1]))
                sp.wait_ge(f_free[1], f_count(f, F_PAIR[2 * g + 1] + 1))
                if g == 1:
                    sp.wait_ge(s_full[1], s_max(f, 0, 7) + 1)
                for tile, rows, which, part, done in (
                    (km, 0, K, HI, keys_moved), (qm, 0, Q, HI, keys_moved),
                    (qa, 0, Q, HI, moved), (qa, DH, Q, HI, moved), (qb, 0, Q, LO, moved),
                    (ka, 0, K, HI, moved), (ka, DH, K, LO, moved),
                ):
                    for odd in range(2):
                        src = slab[DH * odd:DH * odd + DH, which, part, :, :]
                        if tile is qm:
                            dst = qm[0:DH, odd:4:2, :]
                        else:
                            dst = tile[rows:rows + DH, p, 4 * g + odd:4 * g + 4:2, :]
                        sp.dma_start(dst, src).then_inc(done[g], 16)

            def move_maxima(f, p, g):
                sp.wait_ge(m_free, m_max(f, g) + 1)
                row = qb[DH + 1:DH + 2, p, 4 * g:4 * g + 4, :].rearrange("o h (t n) -> o (h t) n", t=NT)
                sp.dma_start(row, m_row[:, :]).then_inc(max_moved, 16)

            def store(b, p):
                sp.wait_ge(o_free, O_USES * (b + 1))
                sp.dma_start(out[b].rearrange("(t p) f -> p t f", p=P), x1[:, p]).then_inc(stored, 16)

            def first():
                load_x(0)
                sp.dma_start(ident[:], identity).then_inc(raw_loaded[0], 16)
                sp.dma_start(mask_rows, nodemask.rearrange("b (t p) -> (b t) p", p=P)).then_inc(raw_loaded[0], 16)
                load_adj(0)
                sp.dma_start(raw_k0, k0.rearrange("(t p) n -> p t n", p=P)).then_inc(raw_loaded[3], 16)
                sp.dma_start(raw_qkv, w_qkv.rearrange("(k p) n -> p k n", p=P)).then_inc(raw_loaded[1], 16)
                sp.dma_start(raw_out, w_out.rearrange("(t p) n -> p t n", p=P)).then_inc(raw_loaded[2], 16)
                sp.dma_start(b_bc[:], b_out.unsqueeze(0).to_broadcast([P, D])).then_inc(raw_loaded[4], 16)
                sp.wait_ge(ones_ready, 1)
                for dst, rows in ((km[DH:DH + 2], 2), (qb[DH:DH + 1], 1)):
                    sp.dma_start(dst.rearrange("p a h (r n) -> p (a h r) n", n=P),
                                 ones[0:rows, :].unsqueeze(1).to_broadcast([rows, 2 * HEADS * NT, P]),
                                 ).then_inc(ones_placed, 16)
                sp.dma_start(qm[DH:DH + 1].rearrange("p h (r n) -> p (h r) n", n=P),
                             ones[0:1, :].unsqueeze(1).to_broadcast([1, 4 * NT, P])).then_inc(ones_placed, 16)
                sp.wait_ge(mask_biased, 1)
                sp.dma_start(bias_rows.rearrange("b (t p) -> (b t) p", p=P), mask_bias).then_inc(bias_stored, 16)
                sp.wait_ge(bias_stored, 16)
                sp.wait_ge(ones_placed, 48)
                load_adj(1)
                load_x(1)
                move_mask_bias(0, 0)
                move_heads(0, 0, 0)
                move_maxima(0, 0, 0)
                move_heads(0, 0, 1)

            def body(b, p):
                if after_first(b):
                    store(b - 1, 1 - p)
                move_maxima(b, p, 1)
                if has_front(b):
                    move_mask_bias(b + 1, 1 - p)
                    move_heads(b + 1, 1 - p, 0)
                if has_load(b):
                    load_x(b + 2)
                if has_front(b):
                    move_maxima(b + 1, 1 - p, 0)
                    move_heads(b + 1, 1 - p, 1)
                if has_load(b):
                    load_adj(b + 2)

            entries(sp, body, first)
            store(B - 1, (B - 1) % 2)
            sp.wait_ge(stored, 16 * B)

        @block.tensor
        def _(pe):
            def split_mm(dst, lhs, rhs, tiles, open_group=True, close_group=True):
                steps = [(i, a, c) for i in range(tiles) for a, c in PRODUCTS]
                for n, (i, a, c) in enumerate(steps):
                    last = nc.tensor.matmul(dst, lhs(a, i), rhs(c, i), start=open_group and n == 0,
                                            stop=close_group and n == len(steps) - 1)
                return last

            def f_bank(f, i):
                wait(pe, f_free[i % 2], F_USES // 2 * f + i // 2)
                return f_ps[:, i % 2, :]

            def both_evacuated(f, i):
                pe.wait_ge(f_free[0], f_count(f, i - 1))
                pe.wait_ge(f_free[1], f_count(f, i))

            def adj_transposes(f, jt):
                if jt == 0:
                    pe.wait_ge(adj_loaded, 16 * (f + 1))
                bank = f_bank(f, F_ADJ + jt)
                for it in range(NT):
                    last = nc.tensor.transpose(bank[:, it * P:(it + 1) * P],
                                               adj_sb[:, it, jt * P:(jt + 1) * P], ident[:])
                last.then_inc(f_full, 1)

            def adj_h1(f, ft):
                if ft == 0:
                    both_evacuated(f, F_T - 1)
                    pe.wait_ge(h_lo, 2 * f + 1)
                bank = f_bank(f, F_T + ft)
                split_mm(bank, lambda a, i: h_s[:, a, i, ft * P:(ft + 1) * P],
                         lambda c, i: adjT[:, c, i, :], NT).then_inc(f_full, 1)

            def t_kernel(f, half):
                if half == 0:
                    both_evacuated(f, F_Y - 1)
                bank = f_bank(f, F_Y + half)
                for k in range(2):
                    it = 2 * half + k
                    last = split_mm(bank[:, k * D:(k + 1) * D],
                                    lambda a, i: hT[:, a, i, it * P:(it + 1) * P],
                                    lambda c, i: wk0[:, c, i, :], KT)
                last.then_inc(f_full, 1)

            def h2_transposes(f, it):
                pe.wait_ge(ln_relu, 2 * NT * f + NT + it + 1)
                for ft in range(KT):
                    bank = f_bank(f, F_H2 + ft) if it == 0 else f_ps[:, (F_H2 + ft) % 2, :]
                    last = nc.tensor.transpose(bank[:, it * P:(it + 1) * P],
                                               h_f[:, it, ft * P:(ft + 1) * P], ident[:])
                    if it == NT - 1:
                        last.then_inc(f_full, 1)

            def queries_keys(f, pair, which):
                if pair == 0 and which == Q:
                    both_evacuated(f, F_H2 + 1)
                bank = f_bank(f, F_PAIR[pair] + which)
                split_mm(bank, lambda a, i: wqkv[:, a, i, which, pair * P:(pair + 1) * P],
                         lambda c, i: hT[:, c, i, :], KT).then_inc(f_full, 1)

            def values(f, jt):
                bank = f_bank(f, F_V + jt)
                split_mm(bank, lambda a, i: hT[:, a, i, jt * P:(jt + 1) * P],
                         lambda c, i: wqkv[:, c, i, V, :], KT).then_inc(f_full, 1)

            def u_product(f, ft):
                if ft == 0:
                    pe.wait_ge(g_lo, NT * (f + 1))
                    pe.wait_ge(h_lo, 2 * f + 2)
                bank = f_bank(f, F_U + ft)
                split_mm(bank, lambda a, i: h_s[:, a, i, ft * P:(ft + 1) * P],
                         lambda c, i: gT[:, c, i, :], NT).then_inc(f_full, 1)

            def blend_row(f):
                pe.wait_ge(mean_ready, f + 1)
                wait(pe, m_free, m_blend(f))
                split_mm(m_ps[:, 0:D], lambda a, i: mean_rep[:, a, i, :],
                         lambda c, i: wc[:, c, i, :], KT).then_inc(m_full, 1)

            def maxima_step(f, p, g, j):
                h = 4 * g + j // 2
                if j == 0:
                    if g == 0:
                        pe.wait_ge(bias_moved, 16 * (f + 1))
                    pe.wait_ge(keys_moved[g], 4 * 16 * (f + 1))
                wait(pe, s_free[j % 2], s_max(f, g, j))
                for k in range(2):
                    it = 2 * (j % 2) + k
                    last = nc.tensor.matmul(s_ps[:, j % 2, k, :], qm[0:DH + 1, h % 4, it * P:(it + 1) * P],
                                            km[0:DH + 1, p, h, :], start=True, stop=True)
                last.then_inc(s_full[j % 2], 1)

            def maxima_transpose(f, g):
                pe.wait_ge(s_free[1], s_max(f, g, 7) + 1)
                wait(pe, m_free, m_max(f, g))
                nc.tensor.transpose(m_ps[0:HEADS // 2 * NT, 0:P],
                                    maxima[:, 4 * g:4 * g + 4, :].rearrange("p h t -> p (h t)"),
                                    ident[:]).then_inc(m_full, 1)

            def scores(b, p, h, half):
                if h % 4 == 0 and half == 0:
                    g = h // 4
                    pe.wait_ge(moved[g], 10 * 16 * (b + 1))
                    pe.wait_ge(max_moved, 16 * (2 * b + g + 1))
                wait(pe, s_free[half], s_score(b, h, half))
                for k in range(2):
                    cols = slice((2 * half + k) * P, (2 * half + k + 1) * P)
                    nc.tensor.matmul(s_ps[:, half, k, :], ka[:, p, h, cols], qa[:, p, h, :],
                                     start=True, stop=False)
                    last = nc.tensor.matmul(s_ps[:, half, k, :], km[0:DH + 2, p, h, cols],
                                            qb[0:DH + 2, p, h, :], start=False, stop=True)
                last.then_inc(s_full[half], 1)

            def attend(b, p, h, half):
                if half == 0:
                    if h == 0:
                        both_evacuated(b, F_V + NT - 1)
                    wait(pe, o_free, O_USES * b + h)
                pe.wait_ge(p_lo[half], HEADS * b + h + 1)
                for k in range(2):
                    jt = 2 * half + k
                    for it in range(NT):
                        dst = o_ps[:, it * (DH + 1):(it + 1) * (DH + 1)]
                        cols = slice(k * N + it * P, k * N + (it + 1) * P)
                        hi = p_s[:, h % 2, half, HI, cols]
                        lo = p_s[:, h % 2, half, LO, cols]
                        nc.tensor.matmul(dst, hi, vh[:, p, jt, h, 0:DH + 1],
                                         start=jt == 0 and it == 0, stop=False, skip_group_check=True)
                        nc.tensor.matmul(dst[:, 0:DH], hi, vl[:, p, jt, h, :],
                                         start=False, stop=False, skip_group_check=True)
                        last = nc.tensor.matmul(dst, lo, vh[:, p, jt, h, 0:DH + 1],
                                                start=False, stop=jt == NT - 1, skip_group_check=True)
                if half == 1:
                    last.then_inc(o_full, 1)

            def pair_transposes(b, t):
                pe.wait_ge(o_free, O_USES * b + 2 * t + 2)
                wait(pe, m_free, m_pair(b, t))
                for it in range(NT):
                    last = nc.tensor.transpose(m_ps[:, it * P:(it + 1) * P], o_pair[:, it, :], ident[:])
                last.then_inc(m_full, 1)

            def projection(b, it):
                if it % 2 == 0:
                    pe.wait_ge(o_free, O_USES * b + HEADS + it // 2)
                if it == 0:
                    both_evacuated(b, F_U + 1)
                rows = slice(it * P, (it + 1) * P)
                dst = o_ps[:, it % 2 * D:(it % 2 + 1) * D]
                split_mm(dst, lambda a, i: uT[:, a, i, rows], lambda c, i: wc[:, c, i, :], KT,
                         close_group=False)
                if it == 0:
                    pe.wait_ge(m_free, m_pair(b, PAIRS - 1) + 1)
                last = split_mm(dst, lambda a, i: oT[:, a, i, rows], lambda c, i: wo[:, c, i, :],
                                PAIRS, open_group=False)
                if it % 2 == 1:
                    last.then_inc(o_full, 1)

            def first():
                pe.wait_ge(raw_loaded[0], 32)
                pe.wait_ge(mask_cast, 1)
                nc.tensor.transpose(m_ps[:, 0:B * NT], mask_f, ident[0:B * NT, 0:B * NT]).then_inc(mask_turned, 1)
                for jt in range(NT):
                    adj_transposes(0, jt)
                adj_h1(0, 0)
                adj_h1(0, 1)
                pe.wait_ge(wv_gathered, 1)
                for t in range(NT):
                    for kt in range(KT):
                        last = nc.tensor.transpose(
                            s_ps[:, 0, t // 2, (t % 2) * D + kt * P:(t % 2) * D + (kt + 1) * P],
                            raw_v[:, kt, t * P:(t + 1) * P], ident[:])
                last.then_inc(wvT_full, 1)
                pe.wait_ge(kernel_split, 1)
                t_kernel(0, 0)
                t_kernel(0, 1)
                pe.wait_ge(wvT_copied, 1)
                pe.wait_ge(wo_scaled, 1)
                for kt in range(KT):
                    for t in range(NT):
                        last = nc.tensor.matmul(o_ps[:, kt * D:(kt + 1) * D], wvT[:, t, kt * P:(kt + 1) * P],
                                                raw_out[:, t, :], start=t == 0, stop=t == NT - 1)
                last.then_inc(wc_full, 1)
                for it in range(NT):
                    h2_transposes(0, it)
                pe.wait_ge(wc_split, 1)
                pe.wait_ge(qkv_split, 1)
                queries_keys(0, 0, Q)
                queries_keys(0, 0, K)
                queries_keys(0, 1, Q)
                queries_keys(0, 1, K)
                blend_row(0)
                values(0, 0)
                values(0, 1)
                values(0, 2)
                maxima_step(0, 0, 0, 0)
                maxima_step(0, 0, 0, 1)
                values(0, 3)
                for j in range(2, 6):
                    maxima_step(0, 0, 0, j)
                queries_keys(0, 2, Q)
                queries_keys(0, 2, K)
                maxima_step(0, 0, 0, 6)
                queries_keys(0, 3, Q)
                maxima_step(0, 0, 0, 7)
                maxima_transpose(0, 0)
                queries_keys(0, 3, K)

            def body(b, p):
                f, q = b + 1, 1 - p
                front, before = has_front(b), after_first(b)
                if before:
                    attend(b - 1, q, HEADS - 1, 0)
                    attend(b - 1, q, HEADS - 1, 1)
                scores(b, p, 0, 0)
                if before:
                    pair_transposes(b - 1, PAIRS - 1)
                scores(b, p, 0, 1)
                if before:
                    projection(b - 1, 0)
                maxima_step(b, p, 1, 0)
                if before:
                    projection(b - 1, 1)
                scores(b, p, 1, 0)
                maxima_step(b, p, 1, 1)
                if before:
                    projection(b - 1, 2)
                maxima_step(b, p, 1, 2)
                maxima_step(b, p, 1, 3)
                if before:
                    projection(b - 1, 3)
                maxima_step(b, p, 1, 4)
                u_product(b, 0)
                maxima_step(b, p, 1, 5)
                u_product(b, 1)
                maxima_step(b, p, 1, 6)
                if front:
                    adj_transposes(f, 0)
                scores(b, p, 1, 1)
                if front:
                    adj_transposes(f, 1)
                attend(b, p, 0, 0)
                attend(b, p, 0, 1)
                maxima_step(b, p, 1, 7)
                if front:
                    adj_transposes(f, 2)
                    adj_transposes(f, 3)
                scores(b, p, 2, 0)
                maxima_transpose(b, 1)
                scores(b, p, 2, 1)
                attend(b, p, 1, 0)
                scores(b, p, 3, 0)
                if front:
                    adj_h1(f, 0)
                    adj_h1(f, 1)
                attend(b, p, 1, 1)
                scores(b, p, 3, 1)
                if front:
                    t_kernel(f, 0)
                    t_kernel(f, 1)
                scores(b, p, 4, 0)
                attend(b, p, 2, 0)
                attend(b, p, 2, 1)
                pair_transposes(b, 0)
                scores(b, p, 4, 1)
                scores(b, p, 5, 0)
                attend(b, p, 3, 0)
                attend(b, p, 3, 1)
                if front:
                    h2_transposes(f, 0)
                scores(b, p, 5, 1)
                if front:
                    h2_transposes(f, 1)
                    h2_transposes(f, 2)
                    h2_transposes(f, 3)
                attend(b, p, 4, 0)
                scores(b, p, 6, 0)
                attend(b, p, 4, 1)
                if front:
                    queries_keys(f, 0, Q)
                    queries_keys(f, 0, K)
                pair_transposes(b, 1)
                if front:
                    queries_keys(f, 1, Q)
                    queries_keys(f, 1, K)
                scores(b, p, 6, 1)
                scores(b, p, 7, 0)
                if front:
                    values(f, 0)
                    blend_row(f)
                attend(b, p, 5, 0)
                scores(b, p, 7, 1)
                attend(b, p, 5, 1)
                if front:
                    maxima_step(f, q, 0, 0)
                    maxima_step(f, q, 0, 1)
                    values(f, 1)
                    maxima_step(f, q, 0, 2)
                    values(f, 2)
                    maxima_step(f, q, 0, 3)
                    maxima_step(f, q, 0, 4)
                    values(f, 3)
                pair_transposes(b, 2)
                attend(b, p, 6, 0)
                if front:
                    maxima_step(f, q, 0, 5)
                    maxima_step(f, q, 0, 6)
                    queries_keys(f, 2, Q)
                    maxima_step(f, q, 0, 7)
                attend(b, p, 6, 1)
                if front:
                    queries_keys(f, 2, K)
                    queries_keys(f, 3, Q)
                    maxima_transpose(f, 0)
                    queries_keys(f, 3, K)

            entries(pe, body, first)
            attend(B - 1, (B - 1) % 2, HEADS - 1, 0)
            attend(B - 1, (B - 1) % 2, HEADS - 1, 1)
            pair_transposes(B - 1, PAIRS - 1)
            projection(B - 1, 0)
            projection(B - 1, 1)
            projection(B - 1, 2)
            projection(B - 1, 3)

        @block.scalar
        def _(act):
            def relu_norm(f, p, layer, half):
                act.wait_ge(ln_bias, 2 * f + layer + 1)
                src = xin if layer == 0 else x1[:, p]
                if layer == 0 and half == 0:
                    wait(act, f_full, F_USES * (f - 1) + F_H2 + 2)
                    wait(act, h_lo, 2 * f)
                for t in (2 * half, 2 * half + 1):
                    nc.scalar.activation(h_f[:, t, :], src[:, t, :], ACT.Relu, bias=nbias[:, t:t + 1],
                                         scale=rstd[:, t:t + 1],
                                         accum_out=h_sum[:, t:t + 1] if layer == 0 else None,
                                         ).then_inc(ln_relu, 1)

            def split_hi(f, i, dst, scale=1.0, **more):
                act.wait_ge(f_full, F_USES * f + i + 1)
                nc.scalar.activation(dst, f_ps[:, i % 2, :], ACT.Copy, scale=scale, **more).then_inc(f_hi, 1)

            def adj_parts(f, p, jt):
                if jt == 0:
                    act.wait_ge(par_ready, f + 1)
                i = F_ADJ + jt
                act.wait_ge(f_full, F_USES * f + i + 1)
                nc.scalar.activation(adjT[:, HI, jt, :], f_ps[:, i % 2, :], ACT.Copy)
                wait(act, g_lo, NT * f + jt - 1)
                nc.scalar.activation(e_sb[:, jt % 2, :], f_ps[:, i % 2, :], ACT.Exp, scale=-1.0,
                                     bias=par[:, p, 1, jt:jt + 1]).then_inc(f_hi, 1)

            def hi_t(f, ft):
                split_hi(f, F_T + ft, hT[:, HI, ft, :])

            def relu_y(f, half):
                if half == 0:
                    act.wait_ge(row_used_ready, f + 1)
                i = F_Y + half
                act.wait_ge(f_full, F_USES * f + i + 1)
                for k in range(2):
                    it = 2 * half + k
                    last = nc.scalar.activation(h_f[:, it, :], f_ps[:, i % 2, k * D:(k + 1) * D], ACT.Relu,
                                                scale=row_used[:, it:it + 1])
                last.then_inc(f_free[i % 2], 1)

            def hi_h2T(f, ft):
                split_hi(f, F_H2 + ft, hT[:, HI, ft, :], accum_out=f_sum[:, ft:ft + 1])

            def hi_pair(f, pair, which):
                if pair == 0 and which == Q:
                    wait(act, moved[1], 10 * 16 * f)
                    wait(act, keys_moved[1], 4 * 16 * f)
                if pair == 2 and which == Q:
                    act.wait_ge(moved[0], 10 * 16 * (f + 1))
                    act.wait_ge(keys_moved[0], 4 * 16 * (f + 1))
                split_hi(f, F_PAIR[pair] + which, slab[:, which, HI, pair % 2, :], scale=1 / W_SCALE)

            def hi_values(f, p, jt):
                i = F_V + jt
                act.wait_ge(f_full, F_USES * f + i + 1)
                nc.scalar.activation(vh[:, p, jt, :, 0:DH],
                                     f_ps[:, i % 2, :].rearrange("p (h d) -> p h d", d=DH),
                                     ACT.Copy, scale=1 / W_SCALE).then_inc(f_hi, 1)

            def hi_u(f, ft):
                split_hi(f, F_U + ft, uT[:, HI, ft, :])

            def negate_maxima(f, g):
                act.wait_ge(m_full, m_max(f, g) + 1)
                wait(act, max_moved, 16 * (2 * f + g))
                nc.scalar.activation(m_row[:, :], m_ps[0:HEADS // 2 * NT, 0:P], ACT.Copy,
                                     scale=-1.0).then_inc(m_free, 1)

            def exponentials(b, h, half):
                act.wait_ge(s_full[half], s_score(b, h, half) + 1)
                wait(act, p_lo[half], HEADS * b + h)
                nc.scalar.activation(p_f[:, half, :].rearrange("p (k n) -> p k n", k=2), s_ps[:, half],
                                     ACT.Exp, scale=DH ** -0.5).then_inc(s_free[half], 1)

            def p_high(b, h, half):
                wait(act, o_full, before_head(b, h))
                act.wait_ge(s_free[half], s_score(b, h, half) + 1)
                nc.scalar.activation(p_s[:, h % 2, half, HI, :], p_f[:, half, :],
                                     ACT.Copy).then_inc(p_hi[half], 1)

            def hi_pair_out(b, t):
                act.wait_ge(m_full, m_pair(b, t) + 1)
                nc.scalar.activation(oT[:, HI, t, :], m_ps[:], ACT.Copy).then_inc(m_hi, 1)

            def first():
                relu_norm(0, 0, 0, 0)
                adj_parts(0, 0, 0)
                adj_parts(0, 0, 1)
                relu_norm(0, 0, 0, 1)
                adj_parts(0, 0, 2)
                adj_parts(0, 0, 3)
                act.wait_ge(raw_loaded[1], 16)
                for kt in range(KT):
                    src = raw_qkv[:, kt, :].rearrange("p (h three d) -> p h three d", three=3, d=DH)
                    last = nc.scalar.activation(raw_v[:, kt, :].rearrange("p (h d) -> p h d", d=DH),
                                                src[:, :, V, :], ACT.Copy)
                last.then_inc(wv_gathered, 1)
                for kt in range(KT):
                    for which in (Q, K, V):
                        src = raw_qkv[:, kt, :].rearrange("p (h three d) -> p h three d", three=3, d=DH)
                        last = nc.scalar.activation(
                            wqkv[:, HI, kt, which, :].rearrange("p (h d) -> p h d", d=DH),
                            src[:, :, which, :], ACT.Copy, scale=W_SCALE)
                last.then_inc(qkv_high, 1)
                hi_t(0, 0)
                hi_t(0, 1)
                act.wait_ge(wvT_full, 1)
                nc.scalar.activation(wvT.rearrange("p (a t) n -> p a (t n)", a=2), s_ps[:, 0],
                                     ACT.Copy).then_inc(wvT_copied, 1)
                relu_y(0, 0)
                relu_y(0, 1)
                act.wait_ge(wc_full, 1)
                nc.scalar.activation(wc[:, HI], o_ps[:].rearrange("p (k n) -> p k n", k=KT),
                                     ACT.Copy).then_inc(wc_high, 1)
                relu_norm(0, 0, 1, 0)
                relu_norm(0, 0, 1, 1)
                hi_h2T(0, 0)
                hi_h2T(0, 1)
                hi_pair(0, 0, Q)
                hi_pair(0, 0, K)
                hi_pair(0, 1, Q)
                hi_pair(0, 1, K)
                hi_values(0, 0, 0)
                hi_values(0, 0, 1)
                hi_values(0, 0, 2)
                hi_values(0, 0, 3)
                hi_pair(0, 2, Q)
                hi_pair(0, 2, K)
                hi_pair(0, 3, Q)
                negate_maxima(0, 0)
                hi_pair(0, 3, K)

            def body(b, p):
                f, q = b + 1, 1 - p
                front, before = has_front(b), after_first(b)
                if before:
                    hi_pair_out(b - 1, PAIRS - 1)
                exponentials(b, 0, 0)
                exponentials(b, 0, 1)
                p_high(b, 0, 0)
                p_high(b, 0, 1)
                exponentials(b, 1, 0)
                p_high(b, 1, 0)
                if front:
                    relu_norm(f, q, 0, 0)
                    relu_norm(f, q, 0, 1)
                hi_u(b, 0)
                hi_u(b, 1)
                if front:
                    adj_parts(f, q, 0)
                    adj_parts(f, q, 1)
                exponentials(b, 1, 1)
                p_high(b, 1, 1)
                if front:
                    adj_parts(f, q, 2)
                    adj_parts(f, q, 3)
                exponentials(b, 2, 0)
                negate_maxima(b, 1)
                p_high(b, 2, 0)
                exponentials(b, 2, 1)
                exponentials(b, 3, 0)
                if front:
                    hi_t(f, 0)
                    hi_t(f, 1)
                p_high(b, 3, 0)
                exponentials(b, 3, 1)
                if front:
                    relu_y(f, 0)
                    relu_y(f, 1)
                exponentials(b, 4, 0)
                p_high(b, 4, 0)
                hi_pair_out(b, 0)
                exponentials(b, 4, 1)
                if front:
                    relu_norm(f, q, 1, 0)
                    relu_norm(f, q, 1, 1)
                exponentials(b, 5, 0)
                if front:
                    hi_h2T(f, 0)
                    hi_h2T(f, 1)
                p_high(b, 5, 0)
                exponentials(b, 5, 1)
                if front:
                    hi_pair(f, 0, Q)
                p_high(b, 5, 1)
                if front:
                    hi_pair(f, 0, K)
                exponentials(b, 6, 0)
                if front:
                    hi_pair(f, 1, Q)
                hi_pair_out(b, 1)
                if front:
                    hi_pair(f, 1, K)
                exponentials(b, 6, 1)
                p_high(b, 6, 1)
                exponentials(b, 7, 0)
                if front:
                    hi_values(f, q, 0)
                exponentials(b, 7, 1)
                if front:
                    hi_values(f, q, 1)
                p_high(b, 7, 0)
                if front:
                    hi_values(f, q, 2)
                    hi_values(f, q, 3)
                hi_pair_out(b, 2)
                p_high(b, 7, 1)
                if front:
                    hi_pair(f, 2, Q)
                    hi_pair(f, 2, K)
                    negate_maxima(f, 0)
                    hi_pair(f, 3, Q)
                    hi_pair(f, 3, K)

            entries(act, body, first)
            hi_pair_out(B - 1, PAIRS - 1)

        @block.vector
        def _(dve):
            def norm_stats(f, p, layer, half):
                if layer == 0:
                    dve.wait_ge(x_loaded, 16 * (f + 1))
                else:
                    dve.wait_ge(y_added, 2 * f + half + 1)
                src = xin if layer == 0 else x1[:, p]
                for t in (2 * half, 2 * half + 1):
                    last = nc.vector.bn_stats(stats[:, t, :], src[:, t, :])
                last.then_inc(ln_stats, 1)

            def norm_var(f, layer):
                k = 2 * f + layer + 1
                dve.wait_ge(ln_stats, 2 * k)
                nc.vector.memset(var_eps[:], EPS)
                for t in range(NT):
                    last = nc.vector.bn_aggr(meanvar[:, t, :], stats[:, t, :])
                last.then_inc(ln_aggr, 1)
                dve.wait_ge(ln_aggr, k)
                nc.vector.tensor_tensor(var_eps[:], meanvar[:, :, 1], var_eps[:], ALU.add).then_inc(ln_var, 1)

            def norm_bias(f, layer):
                dve.wait_ge(ln_rstd, 2 * f + layer + 1)
                nc.vector.scalar_tensor_tensor(nbias[:], meanvar[:, :, 0], -1.0, rstd[:], ALU.mult,
                                               ALU.mult).then_inc(ln_bias, 1)

            def rows_used(f):
                dve.wait_ge(ln_relu, NT * (2 * f + 1))
                nc.vector.tensor_scalar(row_used[:], h_sum[:], 0.0, 1 / K_SCALE, ALU.is_gt,
                                        ALU.mult).then_inc(row_used_ready, 1)

            def h_high(f, layer):
                dve.wait_ge(ln_relu, NT * (2 * f + layer + 1))
                wait(dve, f_full, F_USES * f + (F_T + KT) * layer)
                nc.vector.tensor_copy(h_s[:, HI], h_f[:]).then_inc(h_hi, 1)

            def split_lo(f, i, dst, hi, scale=None):
                dve.wait_ge(f_hi, hi_count(f, i))
                src = f_ps[:, i % 2, :]
                if scale is None:
                    return nc.vector.tensor_tensor(dst, src, hi, ALU.subtract)
                return nc.vector.scalar_tensor_tensor(dst, src, scale, hi, ALU.mult, ALU.subtract)

            def take_par(f, p):
                wait(dve, o_free, O_USES * (f - 1))
                nc.vector.tensor_copy(par[:, p].rearrange("p a t -> p (a t)"),
                                      par_all[:, f].rearrange("p a t -> p (a t)")).then_inc(par_ready, 1)

            def adj_parts(f, p, jt):
                if jt == 0:
                    dve.wait_ge(par_ready, f + 1)
                i = F_ADJ + jt
                split_lo(f, i, adjT[:, LO, jt, :], adjT[:, HI, jt, :])
                e = e_sb[:, jt % 2, :]
                nc.vector.scalar_tensor_tensor(e, f_ps[:, i % 2, :], par[:, p, 0, jt:jt + 1], e,
                                               ALU.mult, ALU.add).then_inc(f_free[i % 2], 1)

            def g_high(f, jt):
                i = F_ADJ + jt
                dve.wait_ge(f_free[i % 2], f_count(f, i))
                nc.vector.tensor_copy(gT[:, HI, jt, :], e_sb[:, jt % 2, :]).then_inc(g_hi, 1)

            def lo_t(f, ft):
                i = F_T + ft
                split_lo(f, i, hT[:, LO, ft, :], hT[:, HI, ft, :]).then_inc(f_free[i % 2], 1)

            def add_y(f, p, half):
                wait(dve, stored, 16 * (f - 1))
                dve.wait_ge(f_free[half], f_count(f, F_Y + half))
                rows = slice(2 * half, 2 * half + 2)
                nc.vector.tensor_tensor(x1[:, p, rows, :], xin[:, rows, :], h_f[:, rows, :],
                                        ALU.add).then_inc(y_added, 1)

            def lo_h2T(f, ft):
                i = F_H2 + ft
                split_lo(f, i, hT[:, LO, ft, :], hT[:, HI, ft, :]).then_inc(f_free[i % 2], 1)

            def mean_parts(f):
                for ft in range(KT):
                    last = nc.vector.tensor_scalar(mean_rep[:, HI, ft, :], ones[:], f_sum[:, ft:ft + 1], None,
                                                   ALU.mult)
                last.then_inc(mean_hi, 1)
                dve.wait_ge(mean_hi, f + 1)
                for ft in range(KT):
                    last = nc.vector.scalar_tensor_tensor(mean_rep[:, LO, ft, :], ones[:], f_sum[:, ft:ft + 1],
                                                          mean_rep[:, HI, ft, :], ALU.mult, ALU.subtract)
                last.then_inc(mean_ready, 1)

            def add_blend(f, p):
                dve.wait_ge(m_full, m_blend(f) + 1)
                dve.wait_ge(b_added, f + 1)
                for it in range(NT):
                    last = nc.vector.scalar_tensor_tensor(x1[:, p, it, :], m_ps[:, 0:D], par[:, p, 3, it:it + 1],
                                                          x1[:, p, it, :], ALU.mult, ALU.add)
                last.then_inc(m_free, 1)

            def lo_pair(f, pair, which):
                i = F_PAIR[pair] + which
                split_lo(f, i, slab[:, which, LO, pair % 2, :], slab[:, which, HI, pair % 2, :],
                         1 / W_SCALE).then_inc(f_free[i % 2], 1)

            def lo_values(f, p, jt):
                i = F_V + jt
                dve.wait_ge(f_hi, hi_count(f, i))
                nc.vector.scalar_tensor_tensor(
                    vl[:, p, jt], f_ps[:, i % 2, :].rearrange("p (h d) -> p h d", d=DH), 1 / W_SCALE,
                    vh[:, p, jt, :, 0:DH], ALU.mult, ALU.subtract).then_inc(f_free[i % 2], 1)

            def lo_u(f, ft):
                i = F_U + ft
                split_lo(f, i, uT[:, LO, ft, :], uT[:, HI, ft, :]).then_inc(f_free[i % 2], 1)

            def take_maxima(f, g, j):
                dve.wait_ge(s_full[j % 2], s_max(f, g, j) + 1)
                its = slice(2 * (j % 2), 2 * (j % 2) + 2)
                nc.vector.reduce_max(maxima[:, 4 * g + j // 2, its], s_ps[:, j % 2],
                                     AX_X).then_inc(s_free[j % 2], 1)

            def p_high(b, h, half):
                wait(dve, o_full, before_head(b, h))
                dve.wait_ge(s_free[half], s_score(b, h, half) + 1)
                nc.vector.tensor_copy(p_s[:, h % 2, half, HI, :], p_f[:, half, :]).then_inc(p_hi[half], 1)

            def p_low(b, h, half):
                dve.wait_ge(p_hi[half], HEADS * b + h + 1)
                nc.vector.tensor_tensor(p_s[:, h % 2, half, LO, :], p_f[:, half, :], p_s[:, h % 2, half, HI, :],
                                        ALU.subtract).then_inc(p_lo[half], 1)

            def divide(b, h):
                dve.wait_ge(o_full, O_USES * b + h + 1)
                o = o_ps[:, 0:NT * (DH + 1)].rearrange("p (t d) -> p t d", t=NT)
                nc.vector.reciprocal(recip[:].unsqueeze(2), o[:, :, DH:DH + 1]).then_inc(recip_done, 1)
                dve.wait_ge(recip_done, HEADS * b + h + 1)
                if h % 2 == 0:
                    if h:
                        dve.wait_ge(m_full, m_pair(b, h // 2 - 1) + 1)
                    else:
                        wait(dve, m_full, m_pair(b - 1, PAIRS - 1) + 1 if after_first(b) else 0)
                nc.vector.tensor_tensor(o_pair[:, :, (h % 2) * DH:(h % 2 + 1) * DH], o[:, :, 0:DH],
                                        recip[:].unsqueeze(2).to_broadcast([P, NT, DH]),
                                        ALU.mult).then_inc(o_free, 1)

            def lo_pair_out(b, t):
                dve.wait_ge(m_hi, PAIRS * b + t + 1)
                nc.vector.tensor_tensor(oT[:, LO, t, :], m_ps[:], oT[:, HI, t, :],
                                        ALU.subtract).then_inc(m_free, 1)

            def add_projection(b, p, half):
                dve.wait_ge(o_full, O_USES * b + HEADS + half + 1)
                for k in range(2):
                    it = 2 * half + k
                    last = nc.vector.scalar_tensor_tensor(x1[:, p, it, :], o_ps[:, k * D:(k + 1) * D],
                                                          par[:, p, 2, it:it + 1], x1[:, p, it, :],
                                                          ALU.mult, ALU.add)
                last.then_inc(o_free, 1)

            def first():
                nc.vector.memset(minus_half[:], -0.5)
                nc.vector.memset(ones[:], 1.0).then_inc(ones_ready, 1)
                dve.wait_ge(raw_loaded[0], 32)
                nc.vector.tensor_copy(mask_f, mask_rows).then_inc(mask_cast, 1)
                norm_stats(0, 0, 0, 0)
                norm_stats(0, 0, 0, 1)
                norm_var(0, 0)
                dve.wait_ge(mask_cast, 1)
                nc.vector.tensor_scalar(mask_bias, mask_f, MASKED, -MASKED, ALU.mult,
                                        ALU.add).then_inc(mask_biased, 1)
                dve.wait_ge(mask_turned, 1)
                m = m_ps[:, 0:B * NT].rearrange("p (b t) -> p b t", t=NT)
                for kind, (a, c) in enumerate(((1.0, 0.0), (GONE, -GONE), (1 / W_SCALE, 0.0),
                                               (-1 / (W_SCALE * N), 1 / (W_SCALE * N)))):
                    last = nc.vector.tensor_scalar(par_all[:, :, kind, :], m, a, c, ALU.mult, ALU.add)
                last.then_inc(columns_ready, 1)
                norm_bias(0, 0)
                dve.wait_ge(columns_ready, 1)
                take_par(0, 0)
                adj_parts(0, 0, 0)
                g_high(0, 0)
                adj_parts(0, 0, 1)
                g_high(0, 1)
                rows_used(0)
                h_high(0, 0)
                for jt in range(2, NT):
                    adj_parts(0, 0, jt)
                    g_high(0, jt)
                dve.wait_ge(raw_loaded[3], 16)
                nc.vector.tensor_scalar(wk0[:, HI], raw_k0, K_SCALE, None, ALU.mult).then_inc(kernel_high, 1)
                dve.wait_ge(kernel_high, 1)
                nc.vector.scalar_tensor_tensor(wk0[:, LO], raw_k0, K_SCALE, wk0[:, HI], ALU.mult,
                                               ALU.subtract).then_inc(kernel_split, 1)
                dve.wait_ge(raw_loaded[2], 16)
                nc.vector.tensor_scalar(raw_out, raw_out, LAMBDA * W_SCALE, None, ALU.mult).then_inc(wo_scaled, 1)
                dve.wait_ge(qkv_high, 1)
                for kt in range(KT):
                    for which in (Q, K, V):
                        src = raw_qkv[:, kt, :].rearrange("p (h three d) -> p h three d", three=3, d=DH)
                        last = nc.vector.scalar_tensor_tensor(
                            wqkv[:, LO, kt, which, :].rearrange("p (h d) -> p h d", d=DH), src[:, :, which, :],
                            W_SCALE, wqkv[:, HI, kt, which, :].rearrange("p (h d) -> p h d", d=DH),
                            ALU.mult, ALU.subtract)
                last.then_inc(qkv_split, 1)
                lo_t(0, 0)
                lo_t(0, 1)
                nc.vector.memset(vh[:, :, :, :, DH:DH + 2], 1.0)
                add_y(0, 0, 0)
                norm_stats(0, 0, 1, 0)
                add_y(0, 0, 1)
                norm_stats(0, 0, 1, 1)
                norm_var(0, 1)
                dve.wait_ge(wo_scaled, 1)
                nc.vector.tensor_copy(wo[:, HI], raw_out).then_inc(wo_high, 1)
                norm_bias(0, 1)
                dve.wait_ge(wo_high, 1)
                nc.vector.tensor_tensor(wo[:, LO], raw_out, wo[:, HI], ALU.subtract)
                dve.wait_ge(wc_high, 1)
                nc.vector.tensor_tensor(wc[:, LO], o_ps[:].rearrange("p (k n) -> p k n", k=KT), wc[:, HI],
                                        ALU.subtract).then_inc(wc_split, 1)
                h_high(0, 1)
                lo_h2T(0, 0)
                lo_h2T(0, 1)
                mean_parts(0)
                lo_pair(0, 0, Q)
                lo_pair(0, 0, K)
                lo_pair(0, 1, Q)
                lo_pair(0, 1, K)
                add_blend(0, 0)
                lo_values(0, 0, 0)
                lo_values(0, 0, 1)
                lo_values(0, 0, 2)
                take_maxima(0, 0, 0)
                take_maxima(0, 0, 1)
                lo_values(0, 0, 3)
                take_maxima(0, 0, 2)
                take_maxima(0, 0, 3)
                take_maxima(0, 0, 4)
                take_maxima(0, 0, 5)
                lo_pair(0, 2, Q)
                take_maxima(0, 0, 6)
                lo_pair(0, 2, K)
                take_maxima(0, 0, 7)
                lo_pair(0, 3, Q)
                lo_pair(0, 3, K)

            def body(b, p):
                f, q = b + 1, 1 - p
                front, before = has_front(b), after_first(b)
                if before:
                    divide(b - 1, HEADS - 1)
                    lo_pair_out(b - 1, PAIRS - 1)
                take_maxima(b, 1, 0)
                if before:
                    add_projection(b - 1, q, 0)
                take_maxima(b, 1, 1)
                if front:
                    norm_stats(f, q, 0, 0)
                if not front:
                    p_low(b, 0, 1)
                if front:
                    norm_stats(f, q, 0, 1)
                    norm_var(f, 0)
                take_maxima(b, 1, 2)
                take_maxima(b, 1, 3)
                if front:
                    norm_bias(f, 0)
                p_low(b, 1, 0)
                take_maxima(b, 1, 4)
                if before:
                    add_projection(b - 1, q, 1)
                lo_u(b, 0)
                if front:
                    rows_used(f)
                take_maxima(b, 1, 5)
                if front:
                    take_par(f, q)
                    h_high(f, 0)
                lo_u(b, 1)
                take_maxima(b, 1, 6)
                if front:
                    adj_parts(f, q, 0)
                    adj_parts(f, q, 1)
                    g_high(f, 0)
                    g_high(f, 1)
                take_maxima(b, 1, 7)
                divide(b, 0)
                if front:
                    adj_parts(f, q, 2)
                    adj_parts(f, q, 3)
                if not front:
                    p_low(b, 1, 1)
                p_low(b, 2, 0)
                p_high(b, 2, 1)
                if front:
                    lo_t(f, 0)
                    lo_t(f, 1)
                divide(b, 1)
                if not front:
                    p_low(b, 2, 1)
                if front:
                    g_high(f, 2)
                p_low(b, 3, 0)
                if front:
                    add_y(f, q, 0)
                p_high(b, 3, 1)
                if front:
                    add_y(f, q, 1)
                    norm_stats(f, q, 1, 0)
                    norm_stats(f, q, 1, 1)
                    norm_var(f, 1)
                divide(b, 2)
                if front:
                    norm_bias(f, 1)
                if not front:
                    p_low(b, 3, 1)
                p_low(b, 4, 0)
                p_high(b, 4, 1)
                divide(b, 3)
                if not front:
                    p_low(b, 4, 1)
                lo_pair_out(b, 0)
                if front:
                    h_high(f, 1)
                    lo_h2T(f, 0)
                    lo_h2T(f, 1)
                    mean_parts(f)
                    lo_pair(f, 0, Q)
                    lo_pair(f, 0, K)
                divide(b, 4)
                if not front:
                    p_low(b, 5, 1)
                p_high(b, 6, 0)
                if front:
                    lo_pair(f, 1, Q)
                    lo_pair(f, 1, K)
                lo_pair_out(b, 1)
                p_low(b, 6, 0)
                if not front:
                    p_low(b, 6, 1)
                if front:
                    g_high(f, 3)
                    add_blend(f, q)
                    lo_values(f, q, 0)
                divide(b, 5)
                if front:
                    take_maxima(f, 0, 0)
                    take_maxima(f, 0, 1)
                    take_maxima(f, 0, 2)
                    lo_values(f, q, 1)
                    take_maxima(f, 0, 3)
                    lo_values(f, q, 2)
                    take_maxima(f, 0, 4)
                    lo_values(f, q, 3)
                    take_maxima(f, 0, 5)
                    take_maxima(f, 0, 6)
                    lo_pair(f, 2, Q)
                lo_pair_out(b, 2)
                if front:
                    take_maxima(f, 0, 7)
                    lo_pair(f, 2, K)
                divide(b, 6)
                if front:
                    lo_pair(f, 3, Q)
                if not front:
                    p_low(b, 7, 1)
                if front:
                    lo_pair(f, 3, K)

            entries(dve, body, first)
            divide(B - 1, HEADS - 1)
            lo_pair_out(B - 1, PAIRS - 1)
            add_projection(B - 1, (B - 1) % 2, 0)
            add_projection(B - 1, (B - 1) % 2, 1)

        @block.gpsimd
        def _(pool):
            def norm_rstd(f, layer):
                pool.wait_ge(ln_var, 2 * f + layer + 1)
                nc.gpsimd.tensor_tensor(rstd[:], var_eps[:], minus_half[:], ALU.pow).then_inc(ln_rstd, 1)

            def h_low(f, layer):
                pool.wait_ge(h_hi, 2 * f + layer + 1)
                nc.gpsimd.tensor_tensor(h_s[:, LO], h_f[:], h_s[:, HI], ALU.subtract).then_inc(h_lo, 1)

            def g_low(f, jt):
                pool.wait_ge(g_hi, NT * f + jt + 1)
                nc.gpsimd.tensor_tensor(gT[:, LO, jt, :], e_sb[:, jt % 2, :], gT[:, HI, jt, :],
                                        ALU.subtract).then_inc(g_lo, 1)

            def add_b(f, p):
                pool.wait_ge(ln_relu, 2 * NT * (f + 1))
                pool.wait_ge(raw_loaded[4], 16)
                nc.gpsimd.tensor_tensor(x1[:, p], x1[:, p], b_bc[:].unsqueeze(1).to_broadcast([P, NT, D]),
                                        ALU.add).then_inc(b_added, 1)

            def p_low(b, h, half):
                pool.wait_ge(p_hi[half], HEADS * b + h + 1)
                nc.gpsimd.tensor_tensor(p_s[:, h % 2, half, LO, :], p_f[:, half, :],
                                        p_s[:, h % 2, half, HI, :], ALU.subtract).then_inc(p_lo[half], 1)

            def first():
                norm_rstd(0, 0)
                g_low(0, 0)
                g_low(0, 1)
                h_low(0, 0)
                g_low(0, 2)
                g_low(0, 3)
                norm_rstd(0, 1)
                h_low(0, 1)
                add_b(0, 0)

            def body(b, p):
                f, q = b + 1, 1 - p
                front = has_front(b)
                p_low(b, 0, 0)
                if front:
                    p_low(b, 0, 1)
                    norm_rstd(f, 0)
                    g_low(f, 0)
                    g_low(f, 1)
                    h_low(f, 0)
                    p_low(b, 1, 1)
                    p_low(b, 2, 1)
                    p_low(b, 3, 1)
                    norm_rstd(f, 1)
                    p_low(b, 4, 1)
                    h_low(f, 1)
                p_low(b, 5, 0)
                if front:
                    p_low(b, 5, 1)
                    add_b(f, q)
                    p_low(b, 6, 1)
                    g_low(f, 2)
                    g_low(f, 3)
                p_low(b, 7, 0)
                if front:
                    p_low(b, 7, 1)

            entries(pool, body, first)


_INS = ["x", "adj", "nodemask", "L0_gnn_kernel", "L1_gnn_W_qkv", "L1_gnn_W_out", "L1_gnn_b_out"]


def kernel(**inputs):
    import numpy as _np
    import concourse.bacc as _bacc
    from concourse import mybir as _mybir
    from concourse.bass_utils import run_bass_kernel_spmd as _run

    nc = _bacc.Bacc("TRN2", target_bir_lowering=False, num_devices=1)
    arrays, args = {}, []
    for name in _INS:
        a = _np.ascontiguousarray(inputs[name])
        if a.dtype == _np.bool_:
            a = a.view(_np.uint8)
        arrays[f"in_{name}"] = a
        args.append(nc.dram_tensor(f"in_{name}", a.shape, _mybir.dt.from_np(a.dtype), kind="ExternalInput").ap())
    eye = _np.eye(128, dtype=_np.float32)
    arrays["in_identity"] = eye
    args.append(nc.dram_tensor("in_identity", eye.shape, _mybir.dt.float32, kind="ExternalInput").ap())
    args.append(nc.dram_tensor("mask_bias_rows", inputs["nodemask"].shape, _mybir.dt.float16).ap())
    args.append(nc.dram_tensor("out_0", inputs["x"].shape, _mybir.dt.float32, kind="ExternalOutput").ap())
    gnn_kernel(nc, *args)
    r = _run(nc, [arrays], core_ids=[0])
    return r.results[0]["out_0"]
```
